# Optimizing a Trainium2 kernel written in Bass

```python
import numpy as np
import jax
import jax.numpy as jnp

def _softmax(x, axis=-1):
    return jax.nn.softmax(x, axis=axis)

def _gelu(x):
    return jax.nn.gelu(x, approximate=True)

def _silu(x):
    return jax.nn.silu(x)

def _sigmoid(x):
    return jax.nn.sigmoid(x)

def _layernorm(x, axis=-1, eps=1e-05):
    m = jnp.mean(x, axis=axis, keepdims=True)
    v = jnp.var(x, axis=axis, keepdims=True)
    return (x - m) / jnp.sqrt(v + eps)

def _scatter_add(tgt, idx, src, axis=0):
    return tgt.at[idx].add(src)

def _segment_sum(src, seg, n):
    return jax.ops.segment_sum(src, seg, n)
kernel_name = 'mk_cond_seq_d1_seqx_r2_df88ae'

def setup_inputs(seed: int=0):
    np.random.seed(seed)
    _w = jnp.asarray

    def _rec_inputs():
        import jax
        import jax.numpy as jnp
        _rk = jax.random.key(seed)
        x = -0.0003929 + 0.9999 * jax.random.normal(jax.random.fold_in(_rk, 1), (2, 2048, 512), jnp.float32)
        _lenS = 2048 - jax.random.randint(jax.random.fold_in(_rk, 7), (2,), 0, max(1, 2048 // 4) + 1, jnp.int32)
        _lenS2 = 2048 - jax.random.randint(jax.random.fold_in(_rk, 8), (2,), 0, max(1, 2048 // 4) + 1, jnp.int32)
        cond_2048 = 0.00782532 + 1.00527 * jax.random.normal(jax.random.fold_in(_rk, 11), (2, 1024), jnp.float32)
        _validS = jnp.arange(2048)[None, :] < _lenS[:, None]
        _validS2 = jnp.arange(2048)[None, :] < _lenS2[:, None]
        _causal = jnp.tril(jnp.ones((2048, 2048), dtype=bool))
        mask_BxS_ik0 = jnp.where(jnp.broadcast_to(_validS[:, :], (2, 2048)), 0, 1).astype(jnp.int32)
        return (x, cond_2048, mask_BxS_ik0)
    x, cond_2048, mask_BxS_ik0 = _rec_inputs()

    def _L0_cond_setup():
        import jax, jax.numpy as jnp
        import numpy as np
        H = 16
        LN_EPS = 1e-05

        def _layernorm(x, scale, bias):
            mu = jnp.mean(x, axis=-1, keepdims=True)
            var = jnp.var(x, axis=-1, keepdims=True)
            return (x - mu) * jax.lax.rsqrt(var + LN_EPS) * scale + bias
        key = jax.random.key(seed)
        ks = jax.random.split(key, 8)
        B, T, D, E = (4, 2048, 512, 1024)
        s = 0.02
        return {'x': jax.random.normal(ks[0], (B, T, D), jnp.float32), 'emb': jax.random.normal(ks[1], (B, E), jnp.float32), 'src_mask': jax.random.randint(ks[2], (B, T), 0, 2).astype(jnp.int32), 'norm_scale': jnp.ones((D,), jnp.float32), 'norm_bias': jnp.zeros((D,), jnp.float32), 'Wq': jax.random.normal(ks[3], (D, D), jnp.float32) * s, 'bq': jnp.zeros((D,), jnp.float32), 'Wk': jax.random.normal(ks[4], (D, D), jnp.float32) * s, 'bk': jnp.zeros((D,), jnp.float32), 'Wv': jax.random.normal(ks[5], (D, D), jnp.float32) * s, 'bv': jnp.zeros((D,), jnp.float32), 'film_emb_W': jax.random.normal(ks[6], (E, 2 * D), jnp.float32) * s, 'film_emb_b': jnp.zeros((2 * D,), jnp.float32), 'film_norm_scale': jnp.ones((D,), jnp.float32), 'film_norm_bias': jnp.zeros((D,), jnp.float32), 'film_out_W': jax.random.normal(ks[7], (D, D), jnp.float32) * s, 'film_out_b': jnp.zeros((D,), jnp.float32)}
    _L0_cond_all = _L0_cond_setup()
    _L0_cond_in = {k: v for k, v in _L0_cond_all.items() if k in ('norm_scale', 'norm_bias', 'Wq', 'bq', 'Wk', 'bk', 'Wv', 'bv', 'film_emb_W', 'film_emb_b', 'film_norm_scale', 'film_norm_bias', 'film_out_W', 'film_out_b')}
    del _L0_cond_all
    return {'x': x, 'cond_2048': cond_2048, 'mask_BxS_ik0': mask_BxS_ik0, 'L0_cond_norm_scale': _L0_cond_in['norm_scale'], 'L0_cond_norm_bias': _L0_cond_in['norm_bias'], 'L0_cond_Wq': _L0_cond_in['Wq'], 'L0_cond_bq': _L0_cond_in['bq'], 'L0_cond_Wk': _L0_cond_in['Wk'], 'L0_cond_bk': _L0_cond_in['bk'], 'L0_cond_Wv': _L0_cond_in['Wv'], 'L0_cond_bv': _L0_cond_in['bv'], 'L0_cond_film_emb_W': _L0_cond_in['film_emb_W'], 'L0_cond_film_emb_b': _L0_cond_in['film_emb_b'], 'L0_cond_film_norm_scale': _L0_cond_in['film_norm_scale'], 'L0_cond_film_norm_bias': _L0_cond_in['film_norm_bias'], 'L0_cond_film_out_W': _L0_cond_in['film_out_W'], 'L0_cond_film_out_b': _L0_cond_in['film_out_b']}

def reference(x, cond_2048, mask_BxS_ik0, L0_cond_norm_scale, L0_cond_norm_bias, L0_cond_Wq, L0_cond_bq, L0_cond_Wk, L0_cond_bk, L0_cond_Wv, L0_cond_bv, L0_cond_film_emb_W, L0_cond_film_emb_b, L0_cond_film_norm_scale, L0_cond_film_norm_bias, L0_cond_film_out_W, L0_cond_film_out_b):
    import jax
    import jax.numpy as jnp

    def _L0_cond_ref(x, emb, src_mask, norm_scale, norm_bias, Wq, bq, Wk, bk, Wv, bv, film_emb_W, film_emb_b, film_norm_scale, film_norm_bias, film_out_W, film_out_b):
        import jax, jax.numpy as jnp
        import numpy as np
        H = 16
        LN_EPS = 1e-05

        def _layernorm(x, scale, bias):
            mu = jnp.mean(x, axis=-1, keepdims=True)
            var = jnp.var(x, axis=-1, keepdims=True)
            return (x - mu) * jax.lax.rsqrt(var + LN_EPS) * scale + bias
        B, T, D = x.shape
        dh = D // H
        xn = _layernorm(x, norm_scale, norm_bias)
        q = xn @ Wq + bq
        k = xn @ Wk + bk
        v = xn @ Wv + bv
        mask = (src_mask == 1)[:, :, None]
        k = jnp.where(mask, -jnp.inf, k)
        v = jnp.where(mask, 0.0, v)
        q = q.reshape(B, T, H, dh).transpose(0, 2, 1, 3)
        k = k.reshape(B, T, H, dh).transpose(0, 2, 1, 3)
        v = v.reshape(B, T, H, dh).transpose(0, 2, 1, 3)
        q = jax.nn.softmax(q, axis=-1)
        k = jax.nn.softmax(k, axis=2)
        attn = jnp.einsum('bhse,bhsd->bhed', k, v)
        y = jnp.einsum('bhtd,bhed->bhte', q, attn)
        y = y.transpose(0, 2, 1, 3).reshape(B, T, D)
        emb_out = jax.nn.silu(emb) @ film_emb_W + film_emb_b
        scale, shift = jnp.split(emb_out, 2, axis=-1)
        h = _layernorm(y, film_norm_scale, film_norm_bias) * (1.0 + scale[:, None, :]) + shift[:, None, :]
        h = jax.nn.silu(h) @ film_out_W + film_out_b
        return x + h
    x = _L0_cond_ref(x, cond_2048, mask_BxS_ik0, L0_cond_norm_scale, L0_cond_norm_bias, L0_cond_Wq, L0_cond_bq, L0_cond_Wk, L0_cond_bk, L0_cond_Wv, L0_cond_bv, L0_cond_film_emb_W, L0_cond_film_emb_b, L0_cond_film_norm_scale, L0_cond_film_norm_bias, L0_cond_film_out_W, L0_cond_film_out_b)
    return x

_drawn_inputs = setup_inputs


def setup_inputs(seed=0):
    import zlib

    import numpy as np

    out = dict(_drawn_inputs(seed))
    spreads = {'L0_cond_norm_scale': (1.0, 0.2),
     'L0_cond_norm_bias': (0.0, 0.1),
     'L0_cond_bq': (0.0, 0.267),
     'L0_cond_bk': (0.0, 0.8),
     'L0_cond_bv': (0.0, 0.1),
     'L0_cond_film_emb_b': (0.0, 0.1),
     'L0_cond_film_norm_scale': (1.0, 0.2),
     'L0_cond_film_norm_bias': (0.0, 0.282),
     'L0_cond_film_out_b': (0.0, 0.1)}
    factors = {}
    for name, (base, spread) in spreads.items():
        noise = np.random.default_rng([zlib.crc32(name.encode()), seed]).standard_normal(out[name].shape)
        drawn = base * np.exp(spread * noise) if base else spread * noise
        out[name] = jnp.asarray(drawn.astype(out[name].dtype))
    for name, factor in factors.items():
        out[name] = (out[name] * factor).astype(out[name].dtype)
    return out
```

```python
import concourse.bass as bass
from concourse import mybir
from contextlib import ExitStack

F32 = mybir.dt.float32
F32R = mybir.dt.float32r
I32 = mybir.dt.int32
ALU = mybir.AluOpType
ACT = mybir.ActivationFunctionType
AX = mybir.AxisListType

P = 128
HEADS = 16
LN_EPS = 1e-5
NEG = -3.0e38
MAX_FLOOR = -1.0e38


def cond_block(nc, x, emb, mask, ns, nb, wq, bq, wk, bk, wv, bv, wf, bf, fs, fb, wo, bo, out):
    B, SEQ, D = x.shape
    E = emb.shape[1]
    TILES = SEQ // P
    C = D // P
    DH = D // HEADS
    HB = P // DH
    EC = E // P
    YC = DH + 1
    GW = HB * YC
    BANK = 512

    x_t = x.rearrange("b (p i) d -> b i p d", i=TILES)
    out_t = out.rearrange("b (p i) d -> b i p d", i=TILES)
    wf_t = wf.rearrange("(p c) n -> c p n", c=EC)

    with ExitStack() as ctx:
        def sb(name, shape, dt=F32):
            return ctx.enter_context(nc.sbuf_tensor(name, shape, dt))

        def sem(name):
            return ctx.enter_context(nc.semaphore(name))

        PS = ctx.enter_context(nc.psum_tensor("PS", [P, 8, BANK], F32))
        Wh = {w: sb(f"W{w}_high", [P, C, D], F32R) for w in "kqvo"}
        Wl = {w: sb(f"W{w}_low", [P, C, D], F32R) for w in "kqvo"}
        z32 = sb("z32", [P, TILES, D])
        k32 = sb("k32", [P, TILES, D])
        eq = sb("eq", [P, TILES, D])
        xs = sb("xs", [P, 2, D])
        zT_h = sb("zT_high", [P, 2, C, P], F32R)
        zT_l = sb("zT_low", [P, 2, C, P], F32R)
        ek_h = sb("ek_high", [P, 2, D], F32R)
        ek_l = sb("ek_low", [P, 2, D], F32R)
        z_h = sb("z_high", [P, 2, D], F32R)
        z_l = sb("z_low", [P, 2, D], F32R)
        R32 = sb("attnT32", [P, C, HB, YC])
        R_h = sb("attnT_high", [P, C, HB, YC], F32R)
        R_l = sb("attnT_low", [P, C, HB, YC], F32R)
        cq_hl = sb("cq_high_low", [P, D], F32R)
        spread = sb("spread", [P, P], F32R)
        colbuf = sb("colbuf", [P, D])
        ck_b = sb("ck_rows", [P, D])
        es = sb("exp_q", [P, D])
        M_b = PS[:, 5, :]
        bo_b = sb("bo_rows", [P, D])
        ident = sb("ident", [P, P])
        same_head = sb("same_head", [P, HB, DH])
        ones = sb("ones", [P, 1])
        half_pow = sb("half_pow", [P, 1])
        eps_c = sb("eps_c", [P, 1])
        VECS = (ns, nb, bv, fs, fb, bf)
        VROWS = len(VECS) * C + C
        vec_c = sb("vec_c", [P, VROWS])
        ns_c, nb_c, bv_c, fs_c, fb_c = (vec_c[:, n * C:(n + 1) * C] for n in range(5))
        bf_c = vec_c[:, 5 * C:VROWS]
        cv_c = sb("cv_c", [P, C])
        emb_wide = sb("emb_zero", [P, EC, 1, B])
        mask_i = sb("mask_i", [P, B, TILES], I32)
        mneg = sb("mask_neg", [P, B, TILES])
        emb_s = sb("emb_s", [P, B, EC])
        emb_g = sb("emb_g", [P, EC, B])
        emb_hl = sb("emb_high_low", [P, EC, 4, B], F32R)
        emb_now = sb("emb_now", [P, 2, 4 * B], F32R)
        filmT_s = sb("film_cols", [P, 2 * C, B])
        filmA = sb("filmA", [P, C, B])
        filmB = sb("filmB", [P, C, B])
        bst = sb("bn_parts", [P, 2, 6])
        mv = sb("mean_var", [P, 2, 2])
        rstd = sb("rstd", [P, 2])
        qm = sb("q_max", [P, 2, HEADS])
        mcol = sb("k_max_col", [P, C])
        rden = sb("rden", [P, C])
        rq = sb("rq", [P, 2, HEADS])

        w_raw = {"k": k32[:, 8:12, :], "q": k32[:, 12:16, :], "v": eq[:, 8:12, :], "o": eq[:, 12:16, :]}
        bkq_b = {"k": z32[:, 8, :], "q": z32[:, 9, :]}
        cq_b = z32[:, 10, :]
        nbB = z32[:, 11, :].rearrange("p (c t) -> p c t", c=C)
        vec_rows = z32[0:VROWS, 12, 0:P]
        film = z32[0:2 * B, 12:14, :]
        y32 = z32[:, 2:4, :]
        yn = z32[:, 4:6, :]
        s32 = z32[:, 6:8, :]
        xb = z32[:, 8:10, :]
        ob = z32[:, 14:16, :]
        Gn = xb

        def y_bank(u):
            return PS[:, 2 * u:2 * u + 2, 0:2 * GW]

        x_in = [sem("x_in_0"), sem("x_in_1")]
        w_in = {w: [sem(f"w{w}_in_{c}") for c in range(C if w in "kq" else 1)] for w in "kqvo"}
        bkq_in, vec_in, emb_in, mask_in, bo_in = (sem(n) for n in ("bkq_in", "vec_in", "emb_in", "mask_in", "bo_in"))
        wf_in = [sem("wf_in_0"), sem("wf_in_1")]
        wf_high, wf_low, emb_s1, embT_ready, film_mm, film_out = (
            sem(n) for n in ("wf_high", "wf_low", "emb_split", "emb_now_s", "film_mm", "film_out"))
        wv_scaled, wv_low = sem("wv_scaled"), sem("wv_low")
        out_st = [sem("out_st_0"), sem("out_st_1")]
        consts, pow_s, ident_s, head_s = sem("consts"), sem("pow_s"), sem("ident_s"), sem("head_s")
        w_high, w_low = sem("w_high"), sem("w_low")
        vecT, vec_ready, nbB_s, cps_done, ckq_s, cv_s = sem("vecT"), sem("vec_ready"), sem("nb_wide_s"), sem("c_ps_done"), sem("ckq_s"), sem("cv_s")
        mneg_s, emb_ready, film_row, filmT, film_ready = (
            sem(n) for n in ("mneg_s", "emb_ready", "film_row", "filmT", "film_ready"))
        mv_ready, ve_s, rstd_ready, z_ready, z_kept, te_kept = (
            sem(n) for n in ("mv_ready", "ve_s", "rstd_ready", "z_ready", "z_kept", "te_kept"))
        t_done, zTh_ready, zTl_ready = sem("t_done"), sem("zTh_ready"), sem("zTl_ready")
        k_done, k_evac, kmax_s, q_done, qmax_s, qsub_s, eq_ready = (
            sem(n) for n in ("k_done", "k_evac", "kmax_s", "q_done", "qmax_s", "qsub_s", "eq_ready"))
        mt1, mcol_s, mbig_s, mt2 = (sem(n) for n in ("mt1", "mcol_s", "mbig_s", "mt2"))
        ks_ready, ek_ready, ekh_s, ekl_ready, zh_ready, zl_ready, acc_s, g_done = (
            sem(n) for n in ("ks_ready", "ek_ready", "ekh_s", "ekl_ready", "zh_ready", "zl_ready", "acc_s", "g_done"))
        g_blk, den_done, rden_ready, gn_ready, gt_done, gth_ready, gtl_ready, at_done, r32_s, rh_s, r_ready = (
            sem(n) for n in ("g_blk", "den_done", "rden_ready", "gn_ready", "gt_done", "gth_ready", "gtl_ready",
                             "at_done", "r32_s", "rh_s", "r_ready"))
        te_done, eTh_ready, eTl_ready, y_done, rq_s, y_evac, mv2_ready, ve2_s, rstd2_ready, yn_ready = (
            sem(n) for n in ("te_done", "eTh_ready", "eTl_ready", "y_done", "rq_s", "y_evac", "mv2_ready",
                             "ve2_s", "rstd2_ready", "yn_ready"))
        ts_done, silu_ready, sh_ready, sl_ready, o_done, xb_ready, o_ready = (
            sem(n) for n in ("ts_done", "silu_ready", "sh_ready", "sl_ready", "o_done", "xb_ready", "o_ready"))

        def need(eng, s, value):
            if not isinstance(value, int) or value > 0:
                eng.wait_ge(s, value)

        def pipeline(eng, first, last, lo, hi, stages, extra={}):
            def step(s):
                if extra.get(s):
                    extra[s]()
                for offset, fn in stages:
                    if 0 <= s + offset < TILES:
                        fn(s + offset, (s + offset) % 2)
            for s in range(first, lo):
                step(s)
            with eng.Fori(lo // 2, hi // 2) as pair:
                for u in range(2):
                    for offset, fn in stages:
                        fn(pair * 2 + (u + offset), (u + offset) % 2)
            for s in range(hi, last):
                step(s)

        P4_STEPS = (-3, TILES + 1, 4, TILES - 4)

        block = ctx.enter_context(nc.Block())

        @block.sync
        def _(sp):
            def load_x(b, i, u):
                sp.dma_start(xs[:, u, :], x_t[b, i]).then_inc(x_in[u], 16)

            def load_w(w, src):
                src = src.rearrange("(c p) n -> p c n", p=P)
                if w in "kq":
                    for c in range(C):
                        sp.dma_start(w_raw[w][:, c, :], src[:, c, :]).then_inc(w_in[w][c], 16)
                else:
                    sp.dma_start(w_raw[w], src).then_inc(w_in[w][0], 16)

            load_x(0, 0, 0)
            load_w("k", wk)
            load_x(0, 1, 1)
            load_w("q", wq)
            load_w("v", wv)
            load_w("o", wo)
            for b in range(B):
                n0 = b * TILES

                def load_p1(i, u):
                    need(sp, t_done, n0 + i - 1)
                    need(sp, z_kept, n0 + i - 1)
                    load_x(b, i, u)

                for i in range(2, 4):
                    load_p1(i, i % 2)
                with sp.Fori(2, TILES // 2) as pair:
                    for u in range(2):
                        load_p1(pair * 2 + u, u)

                if b == 0:
                    for c in range(EC):
                        u = c % 2
                        if c < 2:
                            sp.wait_ge(zl_ready, c + 1)
                            sp.wait_ge(acc_s, c + 1)
                            sp.wait_ge(ekl_ready, c + 1)
                        else:
                            sp.wait_ge(wf_low, c - 1)
                        sp.dma_start(z32[:, u, :], wf_t[c][:, 0:D]).then_inc(wf_in[u], 16)
                        sp.dma_start(k32[:, u, :], wf_t[c][:, D:2 * D]).then_inc(wf_in[u], 16)

                for i in range(2):
                    sp.wait_ge(t_done, n0 + TILES)
                    sp.wait_ge(z_kept, n0 + TILES)
                    load_x(b, i, i)

                def store(i, u):
                    sp.wait_ge(o_ready, n0 + i + 1)
                    sp.dma_start(out_t[b, i], ob[:, u, :]).then_inc(out_st[u], 16)

                def reload(i, u):
                    sp.wait_ge(xb_ready, n0 + i - 1)
                    load_x(b, i, u)

                for i in range(2):
                    reload(i + 2, i)
                    store(i, i)
                with sp.Fori(1, TILES // 2 - 1) as pair:
                    for u in range(2):
                        reload(pair * 2 + (u + 2), u)
                        store(pair * 2 + u, u)
                if b + 1 < B:
                    for i in range(2):
                        sp.wait_ge(xb_ready, n0 + TILES - 1 + i)
                        load_x(b + 1, i, i)
                for i in range(TILES - 2, TILES):
                    store(i, i % 2)
            for u in range(2):
                sp.wait_ge(out_st[u], 16 * B * TILES // 2)

        @block.gpsimd
        def _(pool):
            g = nc.gpsimd
            g.memset(ident[:, :], 0.0).then_inc(ident_s, 1)
            pool.wait_ge(ident_s, 1)
            g.affine_select(out=ident[:, :], in_=ident[:, :], compare_op=ALU.not_equal, fill=1.0, base=0,
                            pattern=[[-1, P]], channel_multiplier=1).then_inc(ident_s, 1)
            g.memset(half_pow[:, :], -0.5).then_inc(pow_s, 1)
            g.memset(eps_c[:, :], LN_EPS).then_inc(pow_s, 1)
            pool.wait_ge(pow_s, 2)
            g.memset(same_head[:, :, :], 1.0).then_inc(head_s, 1)
            pool.wait_ge(head_s, 1)
            g.affine_select(out=same_head[:, :, :], in_=same_head[:, :, :], compare_op=ALU.is_ge, fill=0.0, base=0,
                            pattern=[[-DH, HB], [0, DH]], channel_multiplier=1).then_inc(head_s, 1)
            pool.wait_ge(head_s, 2)
            g.affine_select(out=same_head[:, :, :], in_=same_head[:, :, :], compare_op=ALU.is_ge, fill=0.0,
                            base=DH - 1, pattern=[[DH, HB], [0, DH]], channel_multiplier=-1).then_inc(head_s, 1)

            def w_low_parts(w, high):
                for c in range(C):
                    pool.wait_ge(w_high, high + c + 1)
                    g.tensor_tensor(Wl[w][:, c, :], w_raw[w][:, c, :], Wh[w][:, c, :].bitcast(F32),
                                    ALU.subtract).then_inc(wv_low, 1)

            for b in range(B):
                n0 = b * TILES

                def rstd_p1(i, u):
                    pool.wait_ge(mv_ready, n0 + i + 1)
                    g.tensor_tensor(mv[:, u, 1:2], mv[:, u, 1:2], eps_c[:, :], ALU.add).then_inc(ve_s, 1)
                    pool.wait_ge(ve_s, n0 + i + 1)
                    g.tensor_tensor(rstd[:, u:u + 1], mv[:, u, 1:2], half_pow[:, :], ALU.pow).then_inc(rstd_ready, 1)

                for i in range(6):
                    rstd_p1(i, i % 2)
                if b == 0:
                    w_low_parts("v", 2 * C)
                    rstd_p1(6, 0)
                    w_low_parts("o", 3 * C)
                    rstd_p1(7, 1)
                with pool.Fori(3 + (b == 0), TILES // 2) as pair:
                    for u in range(2):
                        rstd_p1(pair * 2 + u, u)

                def z_low(i, u):
                    pool.wait_ge(zh_ready, n0 + i + 1)
                    g.tensor_tensor(z_l[:, u, :], z32[:, i, :], z_h[:, u, :].bitcast(F32),
                                    ALU.subtract).then_inc(zl_ready, 1)

                def sum_ek(i, u):
                    pool.wait_ge(ek_ready, n0 + i + 1)
                    need(pool, acc_s, n0 + i)
                    g.tensor_tensor(colbuf[:, :], colbuf[:, :], k32[:, i, :], ALU.add).then_inc(acc_s, 1)

                z_low(0, 0)
                pool.wait_ge(mt2, b + 1)
                pool.wait_ge(ek_ready, n0 + 1)
                g.tensor_copy(colbuf[:, :], k32[:, 0, :]).then_inc(acc_s, 1)
                z_low(1, 1)
                sum_ek(1, 1)
                with pool.Fori(1, TILES // 2) as pair:
                    for u in range(2):
                        z_low(pair * 2 + u, u)
                        sum_ek(pair * 2 + u, u)

                def rstd_y(i, u):
                    pool.wait_ge(mv2_ready, n0 + i + 1)
                    g.tensor_tensor(mv[:, u, 1:2], mv[:, u, 1:2], eps_c[:, :], ALU.add).then_inc(ve2_s, 1)
                    pool.wait_ge(ve2_s, n0 + i + 1)
                    g.tensor_tensor(rstd[:, u:u + 1], mv[:, u, 1:2], half_pow[:, :], ALU.pow).then_inc(rstd2_ready, 1)

                def s_low(i, u):
                    pool.wait_ge(sh_ready, n0 + i + 1)
                    g.tensor_tensor(ek_l[:, u, :], s32[:, u, :], ek_h[:, u, :].bitcast(F32),
                                    ALU.subtract).then_inc(sl_ready, 1)

                def residual(i, u):
                    if isinstance(i, int) and i == 0:
                        pool.wait_ge(bo_in, 16)
                    pool.wait_ge(x_in[u], 16 * (b * TILES + TILES // 2 + 1) + 8 * (i - u))
                    need(pool, o_ready, n0 + i - 1)
                    g.tensor_tensor(xb[:, u, :], xs[:, u, :], bo_b[:, :], ALU.add).then_inc(xb_ready, 1)

                pool.wait_ge(gt_done, C * (b + 1))
                pipeline(pool, *P4_STEPS, [(2, rstd_y), (1, s_low), (1, residual)])

        @block.scalar
        def _(act):
            a = nc.scalar
            for n, vec in enumerate(VECS):
                rows = vec.shape[0] // P
                act.dma_start(vec_rows[n * C:n * C + rows, :], vec.rearrange("(c p) -> c p", p=P)).then_inc(vec_in, 16)
            act.dma_start(emb_s[:, :, :], emb.rearrange("b (p c) -> p b c", c=EC)).then_inc(emb_in, 16)
            act.dma_start(bkq_b["k"], bk.partition_broadcast(P)).then_inc(bkq_in, 16)
            act.dma_start(bkq_b["q"], bq.partition_broadcast(P)).then_inc(bkq_in, 16)
            act.dma_start(mask_i[:, :, :], mask.rearrange("b (p i) -> p b i", i=TILES)).then_inc(mask_in, 16)
            act.dma_start(bo_b[:, :], bo.partition_broadcast(P)).then_inc(bo_in, 16)
            act.wait_ge(emb_in, 16)
            for b in range(B):
                a.activation(emb_g[:, :, b], emb_s[:, b, :], ACT.Silu).then_inc(emb_ready, 1)

            def high_parts(w):
                act.wait_ge(vec_ready, 1)
                if w == "v":
                    act.wait_ge(cv_s, 1)
                    for c in range(C):
                        a.activation(w_raw[w][:, c, :], w_raw[w][:, c, :], ACT.Copy,
                                     scale=ns_c[:, c:c + 1]).then_inc(wv_scaled, 1)
                for c in range(C):
                    if w in "kq":
                        act.wait_ge(w_in[w][c], 16)
                        a.activation(Wh[w][:, c, :], w_raw[w][:, c, :], ACT.Copy,
                                     scale=ns_c[:, c:c + 1]).then_inc(w_high, 1)
                    else:
                        if w == "v":
                            act.wait_ge(wv_scaled, c + 1)
                        else:
                            act.wait_ge(w_in[w][0], 16)
                        a.activation(Wh[w][:, c, :], w_raw[w][:, c, :], ACT.Copy).then_inc(w_high, 1)

            for b in range(B):
                n0 = b * TILES

                def zT_high(i, u):
                    act.wait_ge(t_done, n0 + i + 1)
                    need(act, q_done, n0 + i - 1)
                    a.activation(zT_h[:, u, :, :], PS[:, 4 + u, :].rearrange("p (c t) -> p c t", c=C),
                                 ACT.Copy).then_inc(zTh_ready, 1)

                def z_keep(i, u):
                    act.wait_ge(z_ready, n0 + i + 1)
                    a.activation(z32[:, i, :], xs[:, u, :], ACT.Copy).then_inc(z_kept, 1)

                def exp_q(i, u):
                    act.wait_ge(qsub_s, n0 + i + 1)
                    need(act, te_done, n0 + i)
                    a.activation(es[:, :], eq[:, i, :], ACT.Exp).then_inc(eq_ready, 1)

                def eT_keep(i, u):
                    if isinstance(i, int):
                        act.wait_ge(te_done, n0 + i + 1)
                    a.activation(eq[:, i, :], PS[:, 6 + u, :], ACT.Copy).then_inc(te_kept, 1)

                if b == 0:
                    zT_high(0, 0)
                    high_parts("k")
                    z_keep(0, 0)
                    high_parts("q")
                    z_keep(1, 1)
                    zT_high(1, 1)
                    z_keep(2, 0)
                    zT_high(2, 0)
                    exp_q(0, 0)
                    z_keep(3, 1)
                else:
                    zT_high(1, 1)
                    for u in range(2):
                        act.wait_ge(out_st[u], 8 * n0)
                    act.wait_ge(o_done, n0)
                    z_keep(2, 0)
                    zT_high(2, 0)
                    exp_q(0, 0)
                    z_keep(3, 1)

                def p1_step(i, u):
                    if not isinstance(i, int):
                        act.wait_ge(te_done, n0 + i - 1)
                    zT_high(i + 1, 1 - u)
                    exp_q(i - 1, 1 - u)
                    eT_keep(i - 2, u)
                    z_keep(i + 2, u)

                for i in range(2, 6):
                    p1_step(i, i % 2)
                    if b == 0 and i == 3:
                        high_parts("v")
                    if b == 0 and i == 4:
                        high_parts("o")
                with act.Fori(3, TILES // 2 - 1) as pair:
                    for u in range(2):
                        p1_step(pair * 2 + u, u)
                zT_high(TILES - 1, 1)
                exp_q(TILES - 3, 1)
                eT_keep(TILES - 4, 0)
                eT_keep(TILES - 3, 1)

                def exp_k(i, u):
                    act.wait_ge(ks_ready, n0 + i + 1)
                    a.activation(k32[:, i, :], k32[:, i, :], ACT.Exp).then_inc(ek_ready, 1)

                def z_high(i, u):
                    need(act, g_done, n0 + i - 1)
                    a.activation(z_h[:, u, :], z32[:, i, :], ACT.Copy).then_inc(zh_ready, 1)

                def film_high(c, u):
                    act.wait_ge(wf_in[u], 16 * (c - u) + 32)
                    need(act, film_mm, c)
                    if isinstance(c, int) and c == 0:
                        act.wait_ge(q_done, TILES)
                    for half, part in enumerate((z32, k32)):
                        a.activation(zT_h[:, half, :, :], part[:, u, :].rearrange("p (c t) -> p c t", c=C),
                                     ACT.Copy).then_inc(wf_high, 1)

                if b:
                    act.wait_ge(at_done, C * b)
                z_high(0, 0)
                exp_q(TILES - 2, 0)
                exp_k(0, 0)
                z_high(1, 1)
                exp_k(1, 1)
                eT_keep(TILES - 2, 0)
                exp_q(TILES - 1, 1)
                for i in range(2, 4):
                    exp_k(i, i % 2)
                    z_high(i, i % 2)
                eT_keep(TILES - 1, 1)
                if b == 0:
                    for c in range(2):
                        exp_k(c + 4, c)
                        z_high(c + 4, c)
                        film_high(c, c)
                    with act.Fori(1, EC // 2) as pair:
                        for u in range(2):
                            exp_k(pair * 2 + (u + 4), u)
                            z_high(pair * 2 + (u + 4), u)
                            film_high(pair * 2 + u, u)
                with act.Fori(2 + (b == 0) * EC // 2, TILES // 2) as pair:
                    for u in range(2):
                        exp_k(pair * 2 + u, u)
                        z_high(pair * 2 + u, u)
                if b == 0:
                    act.wait_ge(film_mm, EC)
                    act.wait_ge(zl_ready, TILES - 2)
                    for half in range(2):
                        a.activation(film[:, half, :], PS[0:2 * B, 6 + half, :], ACT.Copy).then_inc(film_row, 1)

                act.wait_ge(rden_ready, b + 1)
                if b:
                    act.wait_ge(xb_ready, n0)
                    act.wait_ge(o_ready, n0)

                def scale_g(j):
                    if j < C - 1:
                        act.wait_ge(g_blk, (C - 1) * b + j + 1)
                    else:
                        act.wait_ge(g_done, n0 + TILES)
                    if j >= 2:
                        act.wait_ge(gt_done, C * b + j - 1)
                    a.activation(Gn[:, j % 2, :], PS[:, j, :], ACT.Copy,
                                 scale=rden[:, j:j + 1]).then_inc(gn_ready, 1)

                def gt_high(j):
                    act.wait_ge(gt_done, C * b + j + 1)
                    if j >= 2:
                        act.wait_ge(at_done, C * b + j - 1)
                    else:
                        act.wait_ge(g_done, n0 + TILES)
                    a.activation(z_h[:, j % 2, :], PS[:, 4 + (j + 1) % 2, :], ACT.Copy).then_inc(gth_ready, 1)

                scale_g(0)
                for j in range(C):
                    if j + 1 < C:
                        scale_g(j + 1)
                    gt_high(j)

                def eT_high(i, u):
                    need(act, y_done, n0 + i - 1)
                    if isinstance(i, int) and i < 2:
                        act.wait_ge(q_done, n0 + TILES)
                    a.activation(zT_h[:, u, :, :], eq[:, i, :].rearrange("p (c t) -> p c t", c=C),
                                 ACT.Copy).then_inc(eTh_ready, 1)

                def next_zT():
                    act.wait_ge(z_ready, n0 + TILES + 1)
                    a.activation(z32[:, 0, :], xs[:, 0, :], ACT.Copy).then_inc(z_kept, 1)
                    act.wait_ge(t_done, n0 + TILES + 1)
                    act.wait_ge(y_done, n0 + TILES)
                    a.activation(zT_h[:, 0, :, :], PS[:, 4, :].rearrange("p (c t) -> p c t", c=C),
                                 ACT.Copy).then_inc(zTh_ready, 1)
                    act.wait_ge(z_ready, n0 + TILES + 2)
                    a.activation(z32[:, 1, :], xs[:, 1, :], ACT.Copy).then_inc(z_kept, 1)

                def silu(i, u):
                    act.wait_ge(ts_done, n0 + i + 1)
                    if isinstance(i, int) and i == 0:
                        act.wait_ge(film_ready, 2)
                    need(act, sl_ready, n0 + i - 1)
                    for c in range(C):
                        a.activation(s32[:, u, c * P:(c + 1) * P], PS[:, 6, c * P:(c + 1) * P], ACT.Silu,
                                     bias=filmB[:, c, b:b + 1], scale=filmA[:, c, b:b + 1]).then_inc(silu_ready, 1)

                def s_high(i, u):
                    act.wait_ge(silu_ready, (i + n0 + 1) * C)
                    need(act, o_done, n0 + i - 1)
                    a.activation(ek_h[:, u, :], s32[:, u, :], ACT.Copy).then_inc(sh_ready, 1)

                pipeline(act, *P4_STEPS, [(3, eT_high), (1, silu), (1, s_high)],
                         {TILES - 1: b + 1 < B and next_zT})

        @block.vector
        def _(dve):
            v = nc.vector
            v.memset(ones[:, :], 1.0).then_inc(consts, 1)
            v.memset(R32[:, :, :, :], 0.0).then_inc(r32_s, 1)
            v.memset(nbB[:, :, :], 1.0 / 64).then_inc(nbB_s, 1)
            dve.wait_ge(nbB_s, 1)
            v.tensor_copy(spread[:, :], nbB[:, 0, :]).then_inc(nbB_s, 1)
            dve.wait_ge(nbB_s, 2)

            def stats(b, i, u):
                dve.wait_ge(x_in[u], 16 * (b * TILES + 1) + 8 * (i - u))
                v.bn_stats(bst[:, u, :], xs[:, u, :])
                dve.drain()
                v.bn_aggr(mv[:, u, :], bst[:, u, :]).then_inc(mv_ready, 1)

            def normalize(b, i, u):
                dve.wait_ge(rstd_ready, b * TILES + i + 1)
                v.tensor_scalar(xs[:, u, :], xs[:, u, :], mv[:, u, 0:1], rstd[:, u:u + 1], ALU.subtract,
                                ALU.mult).then_inc(z_ready, 1)

            def zT_low(b, i, u):
                dve.wait_ge(zTh_ready, b * TILES + i + 1)
                v.tensor_tensor(zT_l[:, u, :, :], PS[:, 4 + u, :].rearrange("p (c t) -> p c t", c=C),
                                zT_h[:, u, :, :].bitcast(F32), ALU.subtract).then_inc(zTl_ready, 1)

            def low_parts(w, at):
                for c in range(C):
                    dve.wait_ge(w_high, C * at + c + 1)
                    if w == "o":
                        v.tensor_tensor(Wl[w][:, c, :], w_raw[w][:, c, :], Wh[w][:, c, :].bitcast(F32),
                                        ALU.subtract).then_inc(w_low, 1)
                    else:
                        v.scalar_tensor_tensor(out=Wl[w][:, c, :], in0=w_raw[w][:, c, :], scalar=ns_c[:, c:c + 1],
                                               in1=Wh[w][:, c, :].bitcast(F32), op0=ALU.mult,
                                               op1=ALU.subtract).then_inc(w_low, 1)

            stats(0, 0, 0)
            normalize(0, 0, 0)
            dve.wait_ge(vecT, 1)
            v.tensor_copy(vec_c[:, :], PS[:, 7, 0:VROWS]).then_inc(vec_ready, 1)
            dve.wait_ge(vec_ready, 1)
            for c in range(C):
                v.tensor_copy(nbB[:, c, :], nb_c[:, c:c + 1].broadcast_to([P, P])).then_inc(nbB_s, 1)
            dve.wait_ge(mask_in, 16)
            v.tensor_scalar(mneg[:, :, :], mask_i[:, :, :], 1.0, NEG, ALU.is_equal, ALU.mult).then_inc(mneg_s, 1)
            zT_low(0, 0, 0)
            low_parts("k", 0)
            stats(0, 1, 1)
            normalize(0, 1, 1)
            low_parts("q", 1)
            dve.wait_ge(bkq_in, 32)
            dve.wait_ge(cps_done, 1)
            v.tensor_tensor(ck_b[:, :], PS[:, 6, :], bkq_b["k"], ALU.add).then_inc(ckq_s, 1)
            dve.wait_ge(cps_done, 2)
            v.tensor_tensor(cq_b, PS[:, 7, :], bkq_b["q"], ALU.add).then_inc(ckq_s, 1)
            dve.wait_ge(ckq_s, 2)
            v.tensor_copy(cq_hl[:, :], cq_b).then_inc(ckq_s, 1)
            dve.wait_ge(ckq_s, 3)
            v.tensor_tensor(cq_hl[P // 2:P, :], z32[P // 2:P, 10, :], cq_hl[P // 2:P, :].bitcast(F32),
                            ALU.subtract).then_inc(ckq_s, 1)

            for b in range(B):
                n0 = b * TILES

                def k_out(i, u):
                    dve.wait_ge(k_done, n0 + i + 1)
                    v.scalar_tensor_tensor(out=k32[:, i, :], in0=PS[:, u, :], scalar=mneg[:, b, bass.ds(i, 1)],
                                           in1=ck_b[:, :], op0=ALU.add, op1=ALU.add).then_inc(k_evac, 1)

                def k_max(i, u):
                    dve.wait_ge(k_evac, n0 + i + 1)
                    if isinstance(i, int) and i == 0:
                        if b:
                            dve.wait_ge(den_done, b)
                        v.tensor_copy(colbuf[:, :], k32[:, 0, :]).then_inc(kmax_s, 1)
                    else:
                        dve.wait_ge(kmax_s, n0 + i)
                        v.tensor_tensor(colbuf[:, :], colbuf[:, :], k32[:, i, :], ALU.max).then_inc(kmax_s, 1)

                def q_out(i, u):
                    dve.wait_ge(q_done, n0 + i + 1)
                    q_ps = PS[:, 2 + u, :].rearrange("p (h d) -> p h d", d=DH)
                    v.tensor_reduce(qm[:, u, :], q_ps, axis=AX.X, op=ALU.max).then_inc(qmax_s, 1)
                    dve.wait_ge(qmax_s, n0 + i + 1)
                    v.tensor_tensor(eq[:, i, :].rearrange("p (h d) -> p h d", d=DH), q_ps,
                                    qm[:, u, :].unsqueeze(2).broadcast_to([P, HEADS, DH]),
                                    ALU.subtract).then_inc(qsub_s, 1)

                def k_stage(i, u):
                    k_out(i, u)
                    k_max(i, u)

                if b:
                    zT_low(b, 0, 0)
                    dve.wait_ge(eTl_ready, n0)
                for i in range(2):
                    stats(b, i + 2, i)
                    zT_low(b, i + 1, 1 - i)
                    normalize(b, i + 2, i)
                    k_stage(i, i)
                    q_out(i, i)
                    if b == 0 and i == 0:
                        dve.wait_ge(cv_s, 1)
                        v.tensor_tensor(cv_c[:, :], PS[:, 7, 0:C], bv_c[:, :], ALU.add).then_inc(cv_s, 1)
                        dve.wait_ge(emb_ready, B)
                        v.memset(emb_wide[:, :, :, :], 0.0).then_inc(emb_s1, 1)
                        v.tensor_copy(emb_hl[:, :, 0, :], emb_g[:, :, :]).then_inc(emb_s1, 1)
                        dve.wait_ge(emb_s1, 2)
                        v.tensor_tensor(emb_hl[:, :, 1, :], emb_g[:, :, :], emb_hl[:, :, 0, :].bitcast(F32),
                                        ALU.subtract).then_inc(emb_s1, 1)
                        v.tensor_copy(emb_hl[:, :, 2, :], emb_g[:, :, :]).then_inc(emb_s1, 1)
                        v.tensor_copy(emb_hl[:, :, 3, :], emb_wide[:, :, 0, :]).then_inc(emb_s1, 1)
                with dve.Fori(1, TILES // 2 - 1) as pair:
                    for u in range(2):
                        stats(b, pair * 2 + (u + 2), u)
                        zT_low(b, pair * 2 + (u + 1), 1 - u)
                        normalize(b, pair * 2 + (u + 2), u)
                        k_stage(pair * 2 + u, u)
                        q_out(pair * 2 + u, u)
                zT_low(b, TILES - 1, 1)
                k_stage(TILES - 2, 0)
                k_stage(TILES - 1, 1)

                dve.wait_ge(mt1, b + 1)
                v.tensor_reduce(mcol[:, :], PS[:, 4, :].rearrange("p (c t) -> p c t", c=C), axis=AX.X,
                                op=ALU.max).then_inc(mcol_s, 1)
                dve.wait_ge(mcol_s, b + 1)
                v.tensor_scalar(colbuf[:, :].rearrange("p (c t) -> p c t", c=C),
                                mcol[:, :].unsqueeze(2).broadcast_to([P, C, P]), MAX_FLOOR, None,
                                ALU.max).then_inc(mbig_s, 1)
                q_out(TILES - 2, 0)

                def k_shift(i, u):
                    v.tensor_tensor(k32[:, i, :], k32[:, i, :], M_b[:, :], ALU.subtract).then_inc(ks_ready, 1)

                def ek_split(i, u):
                    dve.wait_ge(ek_ready, n0 + i + 1)
                    need(dve, g_done, n0 + i - 1)
                    v.tensor_copy(ek_h[:, u, :], k32[:, i, :]).then_inc(ekh_s, 1)
                    dve.wait_ge(ekh_s, n0 + i + 1)
                    v.tensor_tensor(ek_l[:, u, :], k32[:, i, :], ek_h[:, u, :].bitcast(F32),
                                    ALU.subtract).then_inc(ekl_ready, 1)

                def film_low(c, u):
                    dve.wait_ge(wf_high, (c + 1) * 2)
                    v.tensor_tensor(zT_l[:, 0, :, :], z32[:, u, :].rearrange("p (c t) -> p c t", c=C),
                                    zT_h[:, 0, :, :].bitcast(F32), ALU.subtract)
                    v.tensor_tensor(zT_l[:, 1, :, :], k32[:, u, :].rearrange("p (c t) -> p c t", c=C),
                                    zT_h[:, 1, :, :].bitcast(F32), ALU.subtract).then_inc(wf_low, 1)
                    v.tensor_copy(emb_now[:, u, :], emb_hl[:, c, :, :].bitcast(F32)
                                  .rearrange("p k b -> p (k b)")).then_inc(embT_ready, 1)

                dve.wait_ge(mt2, b + 1)
                k_shift(0, 0)
                k_shift(1, 1)
                if b:
                    dve.wait_ge(o_done, n0)
                ek_split(0, 0)
                q_out(TILES - 1, 1)
                k_shift(2, 0)
                ek_split(1, 1)
                k_shift(3, 1)
                for i in range(2, 4):
                    ek_split(i, i % 2)
                    k_shift(i + 2, i % 2)
                if b == 0:
                    with dve.Fori(0, EC // 2) as pair:
                        for u in range(2):
                            ek_split(pair * 2 + (u + 4), u)
                            k_shift(pair * 2 + (u + 6), u)
                            film_low(pair * 2 + u, u)
                with dve.Fori(2 + (b == 0) * EC // 2, TILES // 2 - 1) as pair:
                    for u in range(2):
                        ek_split(pair * 2 + u, u)
                        k_shift(pair * 2 + (u + 2), u)
                ek_split(TILES - 2, 0)
                ek_split(TILES - 1, 1)

                dve.wait_ge(den_done, b + 1)
                v.reciprocal(rden[:, :], PS[:, 4, 0:C]).then_inc(rden_ready, 1)
                for j in range(C):
                    dve.wait_ge(gth_ready, C * b + j + 1)
                    v.tensor_tensor(z_l[:, j % 2, :], PS[:, 4 + (j + 1) % 2, :], z_h[:, j % 2, :].bitcast(F32),
                                    ALU.subtract).then_inc(gtl_ready, 1)
                    if b == 0 and j == 0:
                        v.memset(R32[:, :, :, DH:YC], 1.0).then_inc(r32_s, 1)
                        dve.wait_ge(r32_s, 2)
                        dve.wait_ge(head_s, 3)
                        v.tensor_tensor(R32[:, :, :, DH:YC], R32[:, :, :, DH:YC],
                                        same_head[:, :, 0:1].unsqueeze(1).broadcast_to([P, C, HB, 1]),
                                        ALU.mult).then_inc(r32_s, 1)
                    if j:
                        attn_out(j - 1)

                    def attn_out(j):
                        dve.wait_ge(at_done, C * b + j + 1)
                        v.scalar_tensor_tensor(
                            out=R32[:, j, :, 0:DH], in0=PS[:, j, 0:P].rearrange("p (h d) -> p h d", d=DH),
                            scalar=cv_c[:, j:j + 1], in1=same_head[:, :, :], op0=ALU.add,
                            op1=ALU.mult).then_inc(r32_s, 1)
                        dve.wait_ge(r32_s, 3 + C * b + j + 1)
                        if b and j == 0:
                            dve.wait_ge(y_done, n0)
                        v.tensor_copy(R_h[:, j, :, :], R32[:, j, :, :]).then_inc(rh_s, 1)
                        dve.wait_ge(rh_s, C * b + j + 1)
                        v.tensor_tensor(R_l[:, j, :, :], R32[:, j, :, :], R_h[:, j, :, :].bitcast(F32),
                                        ALU.subtract).then_inc(r_ready, 1)
                attn_out(C - 1)
                if b == 0:
                    dve.wait_ge(filmT, 1)
                    fT = PS[:, 6, 0:2 * C * 2 * B].rearrange("p (c k b) -> p c k b", k=2, b=B)
                    v.tensor_tensor(filmT_s[:, :, :], fT[:, :, 0, :],
                                    bf_c.unsqueeze(2).broadcast_to([P, 2 * C, B]), ALU.add).then_inc(film_out, 1)
                    dve.wait_ge(film_out, 1)
                    v.tensor_tensor(filmT_s[:, :, :], filmT_s[:, :, :], fT[:, :, 1, :], ALU.add).then_inc(film_out, 1)
                    dve.wait_ge(film_out, 2)
                    v.scalar_tensor_tensor(out=filmA[:, :, :], in0=filmT_s[:, 0:C, :], scalar=1.0,
                                           in1=fs_c.unsqueeze(2).broadcast_to([P, C, B]), op0=ALU.add,
                                           op1=ALU.mult).then_inc(film_ready, 1)
                    v.scalar_tensor_tensor(out=filmB[:, :, :], in0=filmT_s[:, 0:C, :], scalar=1.0,
                                           in1=fb_c.unsqueeze(2).broadcast_to([P, C, B]), op0=ALU.add,
                                           op1=ALU.mult).then_inc(film_out, 1)
                    dve.wait_ge(film_out, 3)
                    v.tensor_tensor(filmB[:, :, :], filmB[:, :, :], filmT_s[:, C:2 * C, :],
                                    ALU.add).then_inc(film_ready, 1)

                def eT_low(i, u):
                    dve.wait_ge(eTh_ready, n0 + i + 1)
                    v.tensor_tensor(zT_l[:, u, :, :], eq[:, i, :].rearrange("p (c t) -> p c t", c=C),
                                    zT_h[:, u, :, :].bitcast(F32), ALU.subtract).then_inc(eTl_ready, 1)

                def next_z():
                    for i in range(2):
                        stats(b + 1, i, i)
                        normalize(b + 1, i, i)

                def y_out(i, u):
                    dve.wait_ge(y_done, n0 + i + 1)
                    y_ps = y_bank(u).rearrange("p k (h e) -> p k h e", e=YC)
                    v.reciprocal(rq[:, u, :].rearrange("p (k h) -> p k h", k=2), y_ps[:, :, :, DH]).then_inc(rq_s, 1)
                    dve.wait_ge(rq_s, n0 + i + 1)
                    need(dve, ts_done, n0 + i - 1)
                    v.tensor_tensor(y32[:, u, :].rearrange("p (k h e) -> p k h e", k=2, e=DH), y_ps[:, :, :, 0:DH],
                                    rq[:, u, :].rearrange("p (k h) -> p k h", k=2).unsqueeze(3)
                                    .broadcast_to([P, 2, HEADS // 2, DH]), ALU.mult).then_inc(y_evac, 1)
                    dve.wait_ge(y_evac, n0 + i + 1)
                    v.bn_stats(bst[:, u, :], y32[:, u, :])
                    dve.drain()
                    v.bn_aggr(mv[:, u, :], bst[:, u, :]).then_inc(mv2_ready, 1)

                def y_norm(i, u):
                    dve.wait_ge(rstd2_ready, n0 + i + 1)
                    v.tensor_scalar(yn[:, u, :], y32[:, u, :], mv[:, u, 0:1], rstd[:, u:u + 1], ALU.subtract,
                                    ALU.mult).then_inc(yn_ready, 1)

                def result(i, u):
                    dve.wait_ge(o_done, n0 + i + 1)
                    dve.wait_ge(xb_ready, n0 + i + 1)
                    if not isinstance(i, int) or n0 + i >= 2:
                        dve.wait_ge(out_st[u], 8 * (n0 + i - u))
                    v.tensor_tensor(ob[:, u, :], PS[:, 5 + 2 * u, :], xb[:, u, :], ALU.add).then_inc(o_ready, 1)

                pipeline(dve, *P4_STEPS, [(3, eT_low), (2, y_out), (-1, result), (2, y_norm)],
                         {TILES - 1: b + 1 < B and next_z})

        @block.tensor
        def _(pe):
            def three(out_ps, lh, ll, rh, rl, start, stop):
                nc.tensor.matmul(out_ps, lh, rh, start=start, stop=False)
                nc.tensor.matmul(out_ps, lh, rl, start=False, stop=False)
                return nc.tensor.matmul(out_ps, ll, rh, start=False, stop=stop)

            def transposes(bank, src):
                for c in range(C):
                    last = nc.tensor.transpose(PS[:, bank, c * P:(c + 1) * P], src[:, c * P:(c + 1) * P], ident[:, :])
                return last

            def bias_rows(w, bank):
                for c in range(C):
                    pe.wait_ge(w_in[w][c], 16)
                    last = nc.tensor.matmul(PS[:, bank, :], nbB[:, c, :], w_raw[w][:, c, :], start=(c == 0),
                                            stop=(c == C - 1))
                last.then_inc(cps_done, 1)

            def transpose_z(b, i, u):
                pe.wait_ge(z_ready, b * TILES + i + 1)
                need(pe, zTl_ready, b * TILES + i - 1)
                transposes(4 + u, xs[:, u, :]).then_inc(t_done, 1)

            pe.wait_ge(ident_s, 2)
            pe.wait_ge(vec_in, 16 * len(VECS))
            nc.tensor.transpose(PS[:, 7, 0:VROWS], vec_rows, ident[0:VROWS, 0:VROWS]).then_inc(vecT, 1)
            transpose_z(0, 0, 0)

            for b in range(B):
                n0 = b * TILES

                def project_k(i, u):
                    pe.wait_ge(zTl_ready, n0 + i + 1)
                    need(pe, k_evac, n0 + i - 1)
                    for c in range(C):
                        last = three(PS[:, u, :], zT_h[:, u, c, :], zT_l[:, u, c, :], Wh["k"][:, c, :],
                                     Wl["k"][:, c, :], c == 0, c == C - 1)
                    last.then_inc(k_done, 1)

                def project_q(i, u, part=slice(0, C)):
                    if part.start == 0:
                        need(pe, qsub_s, n0 + i - 1)
                        nc.tensor.matmul(PS[:, 2 + u, :], spread[:, :], cq_hl[:, :], start=True, stop=False)
                    for c in range(part.start, part.stop):
                        last = three(PS[:, 2 + u, :], zT_h[:, u, c, :], zT_l[:, u, c, :], Wh["q"][:, c, :],
                                     Wl["q"][:, c, :], False, c == C - 1)
                    if part.stop == C:
                        last.then_inc(q_done, 1)

                def transpose_e(i, u):
                    pe.wait_ge(eq_ready, n0 + i + 1)
                    need(pe, te_kept, n0 + i - 1)
                    transposes(6 + u, es[:, :]).then_inc(te_done, 1)

                if b == 0:
                    pe.wait_ge(nbB_s, 2 + C)
                    bias_rows("k", 6)
                    for c in range(C):
                        pe.wait_ge(w_low, c + 1)
                        if c == 0:
                            pe.wait_ge(zTl_ready, 1)
                        last = three(PS[:, 0, :], zT_h[:, 0, c, :], zT_l[:, 0, c, :], Wh["k"][:, c, :],
                                     Wl["k"][:, c, :], c == 0, c == C - 1)
                    last.then_inc(k_done, 1)
                    transpose_z(0, 1, 1)
                    bias_rows("q", 7)
                    project_k(1, 1)
                    pe.wait_ge(w_low, 2 * C)
                    pe.wait_ge(ckq_s, 4)
                    project_q(0, 0)
                    transpose_z(0, 2, 0)
                    pe.wait_ge(w_in["v"][0], 16)
                    for j in range(C):
                        for c in range(C):
                            last = nc.tensor.matmul(PS[:, 7, j:j + 1], w_raw["v"][:, c, j * P:(j + 1) * P],
                                                    nb_c[:, c:c + 1], start=(c == 0), stop=(c == C - 1))
                    last.then_inc(cv_s, 1)
                    project_q(1, 1)
                    pe.wait_ge(cv_s, 2)
                else:
                    pe.wait_ge(o_ready, n0 - 1)
                    transpose_z(b, 1, 1)
                    project_k(0, 0)
                    project_q(0, 0)
                    transpose_z(b, 2, 0)
                    project_k(1, 1)
                    project_q(1, 1)
                    pe.wait_ge(o_ready, n0)
                    pe.wait_ge(silu_ready, C * n0)
                def p1_step(i, u):
                    transpose_z(b, i + 1, 1 - u)
                    transpose_e(i - 2, u)
                    project_k(i, u)
                    project_q(i, u)

                for i in range(2, 4):
                    p1_step(i, i % 2)
                with pe.Fori(2, TILES // 2 - 1) as pair:
                    for u in range(2):
                        p1_step(pair * 2 + u, u)
                transpose_z(b, TILES - 1, 1)
                transpose_e(TILES - 4, 0)
                project_k(TILES - 2, 0)
                transpose_e(TILES - 3, 1)
                project_k(TILES - 1, 1)
                project_q(TILES - 2, 0)

                pe.wait_ge(kmax_s, n0 + TILES)
                transposes(4, colbuf[:, :]).then_inc(mt1, 1)
                project_q(TILES - 1, 1, slice(0, C // 2))
                pe.wait_ge(mbig_s, b + 1)
                transposes(5, colbuf[:, :]).then_inc(mt2, 1)
                project_q(TILES - 1, 1, slice(C // 2, C))
                transpose_e(TILES - 2, 0)

                def gram(i, u, first=False, final=False):
                    pe.wait_ge(ekl_ready, n0 + i + 1)
                    pe.wait_ge(zl_ready, n0 + i + 1)
                    for j in range(C):
                        cols = slice(j * P, (j + 1) * P)
                        if first and j >= 2:
                            pe.wait_ge(qsub_s, n0 + TILES - 3 + j)
                        last = three(PS[:, j, :], ek_h[:, u, cols], ek_l[:, u, cols], z_h[:, u, :], z_l[:, u, :],
                                     first, final)
                        if final and j < C - 1:
                            last.then_inc(g_blk, 1)
                        if final and j == 1:
                            sum_rows()
                    last.then_inc(g_done, 1)

                def sum_rows():
                    pe.wait_ge(acc_s, n0 + TILES)
                    pe.wait_ge(consts, 1)
                    for j in range(C):
                        last = nc.tensor.matmul(PS[:, 4, j:j + 1], colbuf[:, j * P:(j + 1) * P], ones[:, :],
                                                start=True, stop=True)
                    last.then_inc(den_done, 1)

                def film_rows(c, u):
                    pe.wait_ge(wf_low, c + 1)
                    pe.wait_ge(embT_ready, c + 1)
                    if isinstance(c, int) and c == 0:
                        pe.wait_ge(te_kept, TILES)
                    for half in range(2):
                        rows = PS[0:2 * B, 6 + half, :]
                        nc.tensor.matmul(rows, emb_now[:, u, 0:2 * B],
                                         zT_h[:, half, :, :].rearrange("p c t -> p (c t)"), start=is_first(c), stop=False)
                        last = nc.tensor.matmul(rows, emb_now[:, u, 2 * B:4 * B],
                                                zT_l[:, half, :, :].rearrange("p c t -> p (c t)"), start=False, stop=is_last(c))
                    last.then_inc(film_mm, 1)

                def is_first(c):
                    return isinstance(c, int) and c == 0

                def is_last(c):
                    return isinstance(c, int) and c == EC - 1

                gram(0, 0, first=True)
                transpose_e(TILES - 1, 1)
                for i in range(1, 4):
                    gram(i, i % 2)
                if b == 0:
                    for c in range(2):
                        gram(c + 4, c)
                        film_rows(c, c)
                    with pe.Fori(1, EC // 2 - 1) as pair:
                        for u in range(2):
                            gram(pair * 2 + (u + 4), u)
                            film_rows(pair * 2 + u, u)
                    for c in range(EC - 2, EC):
                        gram(c + 4, c % 2)
                        film_rows(c, c % 2)
                with pe.Fori(2 + (b == 0) * EC // 2, TILES // 2 - 1) as pair:
                    for u in range(2):
                        gram(pair * 2 + u, u)
                gram(TILES - 2, 0)
                gram(TILES - 1, 1, final=True)

                def transpose_g(j):
                    pe.wait_ge(gn_ready, C * b + j + 1)
                    if j >= 2:
                        pe.wait_ge(gtl_ready, C * b + j - 1)
                    transposes(4 + (j + 1) % 2, Gn[:, j % 2, :]).then_inc(gt_done, 1)

                transpose_g(0)
                for j in range(C):
                    if j + 1 < C:
                        transpose_g(j + 1)
                    if b == 0 and j == 0:
                        pe.wait_ge(film_row, 2)
                        for c in range(2 * C):
                            last = nc.tensor.transpose(PS[:, 6, c * 2 * B:(c + 1) * 2 * B],
                                                       film[:, c // C, (c % C) * P:(c % C + 1) * P],
                                                       ident[0:2 * B, 0:2 * B])
                        last.then_inc(filmT, 1)
                    pe.wait_ge(gtl_ready, C * b + j + 1)
                    pe.wait_ge(wv_low, C)
                    cols = slice(j * P, (j + 1) * P)
                    for c in range(C):
                        rows = slice(c * P, (c + 1) * P)
                        last = three(PS[:, j, 0:P], Wh["v"][:, c, cols], Wl["v"][:, c, cols], z_h[:, j % 2, rows],
                                     z_l[:, j % 2, rows], c == 0, c == C - 1)
                    last.then_inc(at_done, 1)
                def attend(i, u):
                    pe.wait_ge(eTl_ready, n0 + i + 1)
                    need(pe, y_evac, n0 + i - 1)
                    for j in range(C):
                        if isinstance(i, int) and i < 2:
                            pe.wait_ge(r_ready, C * b + j + 1)
                            if i == 0 and j < 2 or i == 1 and j < 2:
                                pe.wait_ge(r32_s, 3 + C * b + (4 if i else 2))
                        last = three(y_bank(u)[:, j // 2, (j % 2) * GW:(j % 2 + 1) * GW], zT_h[:, u, j, :],
                                     zT_l[:, u, j, :], R_h[:, j, :, :].rearrange("p h e -> p (h e)"),
                                     R_l[:, j, :, :].rearrange("p h e -> p (h e)"), True, True)
                    last.then_inc(y_done, 1)

                def transpose_y(i, u):
                    pe.wait_ge(yn_ready, n0 + i + 1)
                    need(pe, silu_ready, (i + n0) * C)
                    if b == 0 and isinstance(i, int) and i == 0:
                        pe.wait_ge(film_out, 2)
                    transposes(6, yn[:, u, :]).then_inc(ts_done, 1)

                def project_out(i, u):
                    pe.wait_ge(sl_ready, n0 + i + 1)
                    if b == 0 and isinstance(i, int) and i == 0:
                        pe.wait_ge(wv_low, 2 * C)
                    need(pe, o_ready, n0 + i - 1)
                    for c in range(C):
                        cols = slice(c * P, (c + 1) * P)
                        last = three(PS[:, 5 + 2 * u, :], ek_h[:, u, cols], ek_l[:, u, cols], Wh["o"][:, c, :],
                                     Wl["o"][:, c, :], c == 0, c == C - 1)
                    last.then_inc(o_done, 1)

                pipeline(pe, *P4_STEPS, [(2, attend), (1, transpose_y), (0, project_out)],
                         {TILES - 1: b + 1 < B and (lambda: transpose_z(b + 1, 0, 0))})


_INS = ["x", "cond_2048", "mask_BxS_ik0", "L0_cond_norm_scale", "L0_cond_norm_bias", "L0_cond_Wq", "L0_cond_bq",
        "L0_cond_Wk", "L0_cond_bk", "L0_cond_Wv", "L0_cond_bv", "L0_cond_film_emb_W", "L0_cond_film_emb_b",
        "L0_cond_film_norm_scale", "L0_cond_film_norm_bias", "L0_cond_film_out_W", "L0_cond_film_out_b"]


def kernel(**inputs):
    import numpy as _np
    import concourse.bacc as _bacc
    from concourse.bass_utils import run_bass_kernel_spmd as _run

    nc = _bacc.Bacc("TRN2", target_bir_lowering=False, num_devices=1)
    arrays, args = {}, []
    for name in _INS:
        arr = _np.ascontiguousarray(inputs[name])
        arrays[f"in_{name}"] = arr
        args.append(nc.dram_tensor(f"in_{name}", arr.shape, mybir.dt.from_np(arr.dtype), kind="ExternalInput").ap())
    out = nc.dram_tensor("out_0", inputs["x"].shape, F32, kind="ExternalOutput").ap()
    cond_block(nc, *args, out)
    r = _run(nc, [arrays], core_ids=[0])
    return r.results[0]["out_0"]
```

```python
import concourse.bass as bass
from concourse import mybir
from contextlib import ExitStack

F32 = mybir.dt.float32
F32R = mybir.dt.float32r
I32 = mybir.dt.int32
ALU = mybir.AluOpType
ACT = mybir.ActivationFunctionType
AX = mybir.AxisListType

P = 128
HEADS = 16
LN_EPS = 1e-5
NEG = -3.0e38
MAX_FLOOR = -1.0e38


def cond_block(nc, x, emb, mask, ns, nb, wq, bq, wk, bk, wv, bv, wf, bf, fs, fb, wo, bo, out):
    B, SEQ, D = x.shape
    E = emb.shape[1]
    TILES = SEQ // P
    C = D // P
    DH = D // HEADS
    HB = P // DH
    EC = E // P
    BANK = 512

    x_t = x.rearrange("b (p i) d -> b i p d", i=TILES)
    out_t = out.rearrange("b (p i) d -> b i p d", i=TILES)
    wf_t = wf.rearrange("(p c) n -> c p n", c=EC)

    with ExitStack() as ctx:
        def sb(name, shape, dt=F32):
            return ctx.enter_context(nc.sbuf_tensor(name, shape, dt))

        def sem(name):
            return ctx.enter_context(nc.semaphore(name))

        PS = ctx.enter_context(nc.psum_tensor("PS", [P, 8, BANK], F32))
        Wh = {w: sb(f"W{w}_high", [P, C, D], F32R) for w in "kqvo"}
        Wl = {w: sb(f"W{w}_low", [P, C, D], F32R) for w in "kqvo"}
        z32 = sb("z32", [P, TILES, D])
        k32 = sb("k32", [P, TILES, D])
        eq = sb("eq", [P, TILES, D])
        xs = sb("xs", [P, 2, D])
        zT_h = sb("zT_high", [P, 2, C, P], F32R)
        zT_l = sb("zT_low", [P, 2, C, P], F32R)
        ek_h = sb("ek_high", [P, 2, D], F32R)
        ek_l = sb("ek_low", [P, 2, D], F32R)
        z_h = sb("z_high", [P, 2, D], F32R)
        z_l = sb("z_low", [P, 2, D], F32R)
        R32 = sb("attnT32", [P, C, P])
        R_hl = sb("attnT_high_low", [P, C, 2, P], F32R)
        colbuf = sb("colbuf", [P, D])
        ck_b = sb("ck_rows", [P, D])
        cq_b = sb("cq_rows", [P, D])
        es = sb("exp_q", [P, D])
        M_b = PS[:, 5, :]
        bo_b = sb("bo_rows", [P, D])
        ident = sb("ident", [P, P])
        same_head = sb("same_head", [P, HB, DH])
        ones = sb("ones", [P, P])
        half_pow = sb("half_pow", [P, 1])
        eps_c = sb("eps_c", [P, 1])
        VECS = (ns, nb, bv, fs, fb, bf)
        VROWS = len(VECS) * C + C
        vec_c = sb("vec_c", [P, VROWS])
        ns_c, nb_c, bv_c, fs_c, fb_c = (vec_c[:, n * C:(n + 1) * C] for n in range(5))
        bf_c = vec_c[:, 5 * C:VROWS]
        cv_c = sb("cv_c", [P, C])
        emb_wide = sb("emb_zero", [P, EC, 1, B])
        mask_i = sb("mask_i", [P, B, TILES], I32)
        mneg = sb("mask_neg", [P, B, TILES])
        emb_s = sb("emb_s", [P, B, EC])
        emb_g = sb("emb_g", [P, EC, B])
        emb_hl = sb("emb_high_low", [P, EC, 4, B], F32R)
        emb_now = sb("emb_now", [P, 2, 4 * B], F32R)
        filmT_s = sb("film_cols", [P, 2 * C, B])
        filmA = sb("filmA", [P, C, B])
        filmB = sb("filmB", [P, C, B])
        bst = sb("bn_parts", [P, 4, 6])
        mv = sb("mean_var", [P, 4, 2])
        rstd = sb("rstd", [P, 4])
        qm = sb("q_max", [P, 2, HEADS])
        mcol = sb("k_max_col", [P, C])
        rden = sb("rden", [P, C])
        q_sum = sb("q_sum", [P, 2, HEADS])
        rq = sb("rq", [P, 2, HEADS])

        w_raw = {"k": k32[:, 8:12, :], "q": k32[:, 12:16, :], "v": eq[:, 8:12, :], "o": eq[:, 12:16, :]}
        bkq_b = {"k": z32[:, 8, :], "q": z32[:, 9, :]}
        nbW = {"k": z32[:, 4:8, :], "q": eq[:, 4:8, :], "v": k32[:, 4:8, :]}
        vec_rows = z32[0:2 * C, 12, 0:P]
        vec_rest = z32[0:VROWS - 2 * C, 13, 0:P]
        film = z32[0:2 * B, 12:14, :]
        y32 = z32[:, 2:4, :]
        yn = z32[:, 4:6, :]
        s32 = z32[:, 6:8, :]
        xb = z32[:, 8:10, :]
        y_lo = z32[:, 10:12, :]
        ob = z32[:, 14:16, :]
        Gn = xb

        def y_bank(u):
            return PS[:, 2 * u:2 * u + 2, :].rearrange("p k (j s c) -> p k j s c", j=2, s=2)

        x_in = [sem("x_in_0"), sem("x_in_1")]
        w_in = {w: [sem(f"w{w}_in_{c}") for c in range(C if w in "kq" else 1)] for w in "kqvo"}
        bkq_in, vec_in, emb_in, mask_in, bo_in = (sem(n) for n in ("bkq_in", "vec_in", "emb_in", "mask_in", "bo_in"))
        wf_in = [sem("wf_in_0"), sem("wf_in_1")]
        wf_high, wf_low, emb_s1, embT_ready, film_mm, film_out = (
            sem(n) for n in ("wf_high", "wf_low", "emb_split", "emb_now_s", "film_mm", "film_out"))
        wv_scaled, wv_low = sem("wv_scaled"), sem("wv_low")
        out_st = [sem("out_st_0"), sem("out_st_1")]
        consts, pow_s, ident_s, head_s = sem("consts"), sem("pow_s"), sem("ident_s"), sem("head_s")
        w_high, w_low = sem("w_high"), sem("w_low")
        vec01_in, qsum_s, en_ready, yb_s = sem("vec01_in"), sem("qsum_s"), sem("softmax_q"), sem("y_low_s")
        vecT, vec_ready, nbW_s, nbsum_s, cps_done, ckq_s, cv_s = (
            sem(n) for n in ("vecT", "vec_ready", "nb_times_w", "nb_sum", "c_ps_done", "ckq_s", "cv_s"))
        next_in = [sem("next_x_in_0"), sem("next_x_in_1")]
        mneg_s, emb_ready, film_row, filmT, film_ready = (
            sem(n) for n in ("mneg_s", "emb_ready", "film_row", "filmT", "film_ready"))
        mv_ready, ve_s, rstd_ready, z_ready, z_kept, te_kept = (
            sem(n) for n in ("mv_ready", "ve_s", "rstd_ready", "z_ready", "z_kept", "te_kept"))
        t_done, zTh_ready, zTl_ready = sem("t_done"), sem("zTh_ready"), sem("zTl_ready")
        k_done, k_evac, kmax_s, q_done, q_evac, qmax_s, qsub_s, eq_ready = (
            sem(n) for n in ("k_done", "k_evac", "kmax_s", "q_done", "q_evac", "qmax_s", "qsub_s", "eq_ready"))
        mt1, mcol_s, mbig_s, mt2 = (sem(n) for n in ("mt1", "mcol_s", "mbig_s", "mt2"))
        ks_ready, ek_ready, ekh_s, ekl_ready, zh_ready, zl_ready, acc_s, g_done = (
            sem(n) for n in ("ks_ready", "ek_ready", "ekh_s", "ekl_ready", "zh_ready", "zl_ready", "acc_s", "g_done"))
        g_blk, den_done, rden_ready, gn_ready, gt_done, gth_ready, gtl_ready, at_done, r32_s, rh_s, r_ready = (
            sem(n) for n in ("g_blk", "den_done", "rden_ready", "gn_ready", "gt_done", "gth_ready", "gtl_ready",
                             "at_done", "r32_s", "rh_s", "r_ready"))
        te_done, eTh_ready, eTl_ready, y_done, rq_s, y_evac, mv2_ready, ve2_s, rstd2_ready, yn_ready = (
            sem(n) for n in ("te_done", "eTh_ready", "eTl_ready", "y_done", "rq_s", "y_evac", "mv2_ready",
                             "ve2_s", "rstd2_ready", "yn_ready"))
        ts_done, silu_ready, sh_ready, sl_ready, o_done, xb_ready, o_ready = (
            sem(n) for n in ("ts_done", "silu_ready", "sh_ready", "sl_ready", "o_done", "xb_ready", "o_ready"))

        def heads(ap):
            return ap.rearrange("p (h d) -> p h d", d=DH)

        def per_head(cols):
            return cols.unsqueeze(2).broadcast_to([P, HEADS, DH])

        def need(eng, s, value):
            if not isinstance(value, int) or value > 0:
                eng.wait_ge(s, value)

        def pipeline(eng, first, last, lo, hi, stages, extra={}):
            def step(s):
                if extra.get(s):
                    extra[s]()
                for offset, fn in stages:
                    if 0 <= s + offset < TILES:
                        fn(s + offset, (s + offset) % 2)
            for s in range(first, lo):
                step(s)
            with eng.Fori(lo // 2, hi // 2) as pair:
                for u in range(2):
                    for offset, fn in stages:
                        fn(pair * 2 + (u + offset), (u + offset) % 2)
            for s in range(hi, last):
                step(s)

        FILM_AT = 6
        KEEP_WARM = 13
        P4_LOOP = (4, TILES - 6)
        LOADS = TILES - 1

        def x_arrived(eng, b, i, u, p4):
            eng.wait_ge(x_in[u], 16 * (b * LOADS + p4 * TILES // 2 + 1) + 8 * (i - u))

        def z_at(b, i, u):
            return z32[:, i, :] if b and isinstance(i, int) and i < 2 else xs[:, u, :]

        block = ctx.enter_context(nc.Block())

        @block.sync
        def _(sp):
            def load_x(b, i, u):
                sp.dma_start(xs[:, u, :], x_t[b, i]).then_inc(x_in[u], 16)

            def load_w(w, src):
                src = src.rearrange("(c p) n -> p c n", p=P)
                if w in "kq":
                    for c in range(C):
                        sp.dma_start(w_raw[w][:, c, :], src[:, c, :]).then_inc(w_in[w][c], 16)
                else:
                    sp.dma_start(w_raw[w], src).then_inc(w_in[w][0], 16)

            load_x(0, 0, 0)
            load_x(0, 1, 1)
            load_w("k", wk)
            sp.dma_start(bkq_b["k"], bk.partition_broadcast(P)).then_inc(bkq_in, 16)
            sp.dma_start(mask_i[:, :, :], mask.rearrange("b (p i) -> p b i", i=TILES)).then_inc(mask_in, 16)
            load_w("q", wq)
            sp.dma_start(bkq_b["q"], bq.partition_broadcast(P)).then_inc(bkq_in, 16)
            for b in range(B):
                n0 = b * TILES

                def load_p1(i, u):
                    sp.wait_ge(t_done, n0 + i - 1)
                    sp.wait_ge(z_kept, n0 + i - 1)
                    load_x(b, i, u)

                if b == 0:
                    for i in range(2, 4):
                        load_p1(i, i % 2)
                    load_w("v", wv)
                    for n, vec in enumerate(VECS[2:]):
                        rows = vec.shape[0] // P
                        sp.dma_start(vec_rest[n * C:n * C + rows, :],
                                     vec.rearrange("(c p) -> c p", p=P)).then_inc(vec_in, 16)
                    sp.dma_start(emb_s[:, :, :], emb.rearrange("b (p c) -> p b c", c=EC)).then_inc(emb_in, 16)
                    load_w("o", wo)
                    sp.dma_start(bo_b[:, :], bo.partition_broadcast(P)).then_inc(bo_in, 16)
                with sp.Fori(2, TILES // 2) as pair:
                    for u in range(2):
                        load_p1(pair * 2 + u, u)

                if b == 0:
                    for c in range(EC):
                        u = c % 2
                        if c < 2:
                            sp.wait_ge(zl_ready, c + 1)
                            sp.wait_ge(acc_s, c + 1)
                            sp.wait_ge(ekl_ready, c + 1)
                        else:
                            sp.wait_ge(wf_low, c - 1)
                        sp.dma_start(z32[:, u, :], wf_t[c][:, 0:D]).then_inc(wf_in[u], 16)
                        sp.dma_start(k32[:, u, :], wf_t[c][:, D:2 * D]).then_inc(wf_in[u], 16)

                for i in range(2):
                    sp.wait_ge(t_done, n0 + TILES)
                    sp.wait_ge(z_kept, n0 + TILES)
                    load_x(b, i, i)
                if b + 1 < B:
                    sp.wait_ge(zh_ready, n0 + TILES)
                    sp.wait_ge(zl_ready, n0 + TILES)
                    if b == 0:
                        sp.wait_ge(wf_low, EC)
                    for i in range(2):
                        sp.dma_start(z32[:, i, :], x_t[b + 1, i]).then_inc(next_in[i], 16)

                def store(i, u):
                    sp.wait_ge(o_ready, n0 + i + 1)
                    sp.dma_start(out_t[b, i], ob[:, u, :]).then_inc(out_st[u], 16)

                def reload(i, u):
                    sp.wait_ge(xb_ready, n0 + i - 1)
                    load_x(b, i, u)

                for i in range(2):
                    reload(i + 2, i)
                    store(i, i)
                with sp.Fori(1, TILES // 2 - 1) as pair:
                    for u in range(2):
                        reload(pair * 2 + (u + 2), u)
                        store(pair * 2 + u, u)
                if b + 1 < B:
                    for i in range(2):
                        sp.wait_ge(xb_ready, n0 + TILES - 1 + i)
                        load_x(b + 1, 2 + i, i)
                for i in range(TILES - 2, TILES):
                    store(i, i % 2)
            for u in range(2):
                sp.wait_ge(out_st[u], 16 * B * TILES // 2)

        @block.gpsimd
        def _(pool):
            g = nc.gpsimd
            g.memset(ident[:, :], 0.0).then_inc(ident_s, 1)
            pool.wait_ge(ident_s, 1)
            g.affine_select(out=ident[:, :], in_=ident[:, :], compare_op=ALU.not_equal, fill=1.0, base=0,
                            pattern=[[-1, P]], channel_multiplier=1).then_inc(ident_s, 1)
            g.memset(half_pow[:, :], -0.5).then_inc(pow_s, 1)
            pool.wait_ge(pow_s, 2)
            g.memset(same_head[:, :, :], 1.0).then_inc(head_s, 1)
            pool.wait_ge(head_s, 1)
            g.affine_select(out=same_head[:, :, :], in_=same_head[:, :, :], compare_op=ALU.is_ge, fill=0.0, base=0,
                            pattern=[[-DH, HB], [0, DH]], channel_multiplier=1).then_inc(head_s, 1)
            pool.wait_ge(head_s, 2)
            g.affine_select(out=same_head[:, :, :], in_=same_head[:, :, :], compare_op=ALU.is_ge, fill=0.0,
                            base=DH - 1, pattern=[[DH, HB], [0, DH]], channel_multiplier=-1).then_inc(head_s, 1)

            def w_low_parts(w, high, first):
                for c in range(first, first + C // 2):
                    pool.wait_ge(w_high, high + c + 1)
                    g.tensor_tensor(Wl[w][:, c, :], w_raw[w][:, c, :], Wh[w][:, c, :].bitcast(F32),
                                    ALU.subtract).then_inc(wv_low, 1)

            def nb_sum(n, w, chunks=range(1, C)):
                for c in chunks:
                    pool.wait_ge(nbW_s, n * C + c + 1)
                    pool.wait_ge(nbsum_s, n * (C - 1) + c - 1)
                    g.tensor_tensor(nbW[w][:, 0, :], nbW[w][:, 0, :], nbW[w][:, c, :], ALU.add).then_inc(nbsum_s, 1)

            for b in range(B):
                n0 = b * TILES

                def rstd_x(i, slot):
                    pool.wait_ge(mv_ready, n0 + i + 1)
                    g.tensor_tensor(mv[:, slot, 1:2], mv[:, slot, 1:2], eps_c[:, :], ALU.add).then_inc(ve_s, 1)
                    pool.wait_ge(ve_s, n0 + i + 1)
                    g.tensor_tensor(rstd[:, slot:slot + 1], mv[:, slot, 1:2], half_pow[:, :],
                                    ALU.pow).then_inc(rstd_ready, 1)

                def q_shift(i, u):
                    pool.wait_ge(qmax_s, n0 + i + 1)
                    g.tensor_tensor(heads(eq[:, i, :]), heads(eq[:, i, :]), per_head(qm[:, u, :]),
                                    ALU.subtract).then_inc(qsub_s, 1)

                def q_norm(i, u):
                    pool.wait_ge(rq_s, n0 + i + 1)
                    g.tensor_tensor(heads(es[:, :]), heads(es[:, :]), per_head(rq[:, u, :]),
                                    ALU.mult).then_inc(en_ready, 1)

                if b == 0:
                    rstd_x(0, 0)
                    rstd_x(1, 1)
                    rstd_x(2, 0)
                    nb_sum(1, "q")
                    rstd_x(3, 1)
                    q_shift(0, 0)
                    nb_sum(2, "v", range(1, 2))
                else:
                    rstd_x(2, 0)
                    q_shift(0, 0)
                    rstd_x(3, 1)
                q_norm(0, 0)
                q_shift(1, 1)
                last = 4 if b else 8
                for i in range(2, last):
                    rstd_x(i + 2, i % 2)
                    if b == 0 and i == 2:
                        nb_sum(2, "v", range(2, C))
                    if b == 0 and 3 <= i < 7:
                        w_low_parts("vo"[(i - 3) // 2], ((i - 3) // 2 + 2) * C, (i - 3) % 2 * C // 2)
                    q_norm(i - 1, 1 - i % 2)
                    q_shift(i, i % 2)
                with pool.Fori(last // 2, TILES // 2 - 1) as pair:
                    for u in range(2):
                        rstd_x(pair * 2 + (u + 2), u)
                        q_norm(pair * 2 + (u - 1), 1 - u)
                        q_shift(pair * 2 + u, u)
                q_norm(TILES - 3, 1)

                def z_low(i, u):
                    pool.wait_ge(zh_ready, n0 + i + 1)
                    g.tensor_tensor(z_l[:, u, :], z32[:, i, :], z_h[:, u, :].bitcast(F32),
                                    ALU.subtract).then_inc(zl_ready, 1)

                def sum_ek(i, u):
                    pool.wait_ge(ek_ready, n0 + i + 1)
                    need(pool, acc_s, n0 + i)
                    g.tensor_tensor(colbuf[:, :], colbuf[:, :], k32[:, i, :], ALU.add).then_inc(acc_s, 1)

                z_low(0, 0)
                z_low(1, 1)
                pool.wait_ge(mt2, b + 1)
                pool.wait_ge(ek_ready, n0 + 2)
                g.tensor_tensor(colbuf[:, :], k32[:, 0, :], k32[:, 1, :], ALU.add).then_inc(acc_s, 2)
                with pool.Fori(1, TILES // 2) as pair:
                    for u in range(2):
                        z_low(pair * 2 + u, u)
                        sum_ek(pair * 2 + u, u)

                def rstd_y(i, u):
                    pool.wait_ge(mv2_ready, n0 + i + 1)
                    g.tensor_tensor(mv[:, u, 1:2], mv[:, u, 1:2], eps_c[:, :], ALU.add).then_inc(ve2_s, 1)
                    pool.wait_ge(ve2_s, n0 + i + 1)
                    g.tensor_tensor(rstd[:, u:u + 1], mv[:, u, 1:2], half_pow[:, :], ALU.pow).then_inc(rstd2_ready, 1)

                def s_low(i, u):
                    pool.wait_ge(sh_ready, n0 + i + 1)
                    g.tensor_tensor(ek_l[:, u, :], s32[:, u, :], ek_h[:, u, :].bitcast(F32),
                                    ALU.subtract).then_inc(sl_ready, 1)

                def residual(i, u):
                    if isinstance(i, int) and i == 0:
                        pool.wait_ge(bo_in, 16)
                    x_arrived(pool, b, i, u, True)
                    need(pool, o_ready, n0 + i - 1)
                    g.tensor_tensor(xb[:, u, :], xs[:, u, :], bo_b[:, :], ALU.add).then_inc(xb_ready, 1)

                pool.wait_ge(gt_done, C * (b + 1))
                more = b + 1 < B
                pipeline(pool, -3, TILES - 3, *P4_LOOP, [(1, s_low), (3, rstd_y), (1, residual)],
                         {TILES - 4: more and (lambda: rstd_x(TILES, 2))})
                if more:
                    residual(TILES - 2, 0)
                    s_low(TILES - 2, 0)
                    residual(TILES - 1, 1)
                    rstd_x(TILES + 1, 3)
                    s_low(TILES - 1, 1)
                else:
                    for i in range(TILES - 2, TILES):
                        residual(i, i % 2)

        @block.scalar
        def _(act):
            a = nc.scalar
            for n, vec in enumerate(VECS[:2]):
                act.dma_start(vec_rows[n * C:(n + 1) * C, :],
                              vec.rearrange("(c p) -> c p", p=P)).then_inc(vec01_in, 16)
            act.wait_ge(consts, 1)
            a.activation(eps_c[:, :], ones[:, 0:1], ACT.Copy, scale=LN_EPS).then_inc(pow_s, 1)

            def scale_v():
                act.wait_ge(nbW_s, 3 * C)
                for c in range(C):
                    a.activation(w_raw["v"][:, c, :], w_raw["v"][:, c, :], ACT.Copy,
                                 scale=ns_c[:, c:c + 1]).then_inc(wv_scaled, 1)

            def high_parts(w):
                act.wait_ge(vec_ready, 1)
                for c in range(C):
                    if w in "kq":
                        act.wait_ge(w_in[w][c], 16)
                        a.activation(Wh[w][:, c, :], w_raw[w][:, c, :], ACT.Copy,
                                     scale=ns_c[:, c:c + 1]).then_inc(w_high, 1)
                    else:
                        if w == "v":
                            act.wait_ge(wv_scaled, c + 1)
                        else:
                            act.wait_ge(w_in[w][0], 16)
                        a.activation(Wh[w][:, c, :], w_raw[w][:, c, :], ACT.Copy).then_inc(w_high, 1)

            def nb_times(w):
                for c in range(C):
                    if w == "v" and c == 0:
                        act.wait_ge(w_in[w][0], 16)
                    a.activation(nbW[w][:, c, :], w_raw[w][:, c, :], ACT.Copy,
                                 scale=nb_c[:, c:c + 1]).then_inc(nbW_s, 1)

            for b in range(B):
                n0 = b * TILES

                def zT_high(i, u):
                    act.wait_ge(t_done, n0 + i + 1)
                    need(act, q_done, n0 + i - 1)
                    a.activation(zT_h[:, u, :, :], PS[:, 4 + u, :].rearrange("p (c t) -> p c t", c=C),
                                 ACT.Copy).then_inc(zTh_ready, 1)

                def z_keep(i, u):
                    act.wait_ge(z_ready, n0 + i + 1)
                    a.activation(z32[:, i, :], xs[:, u, :], ACT.Copy).then_inc(z_kept, 1)

                def exp_q(i, u):
                    act.wait_ge(qsub_s, n0 + i + 1)
                    need(act, te_done, n0 + i)
                    a.activation(es[:, :], eq[:, i, :], ACT.Exp).then_inc(eq_ready, 1)

                def eT_keep(i, u):
                    if isinstance(i, int):
                        act.wait_ge(te_done, n0 + i + 1)
                    a.activation(eq[:, i, :], PS[:, 6 + u, :], ACT.Copy).then_inc(te_kept, 1)

                if b == 0:
                    zT_high(0, 0)
                    high_parts("k")
                    z_keep(0, 0)
                    zT_high(1, 1)
                    z_keep(1, 1)
                    high_parts("q")
                    nb_times("k")
                    nb_times("q")
                    z_keep(2, 0)
                    zT_high(2, 0)
                    nb_times("v")
                    act.wait_ge(emb_in, 16)
                    for batch in range(B):
                        a.activation(emb_g[:, :, batch], emb_s[:, batch, :], ACT.Silu).then_inc(emb_ready, 1)
                    exp_q(0, 0)
                    z_keep(3, 1)
                else:
                    act.wait_ge(yn_ready, n0)
                    z_keep(2, 0)
                    zT_high(2, 0)
                    exp_q(0, 0)
                    z_keep(3, 1)

                def p1_step(i, u):
                    zT_high(i + 1, 1 - u)
                    if b == 0 and isinstance(i, int) and i == 2:
                        scale_v()
                    exp_q(i - 1, 1 - u)
                    eT_keep(i - 2, u)
                    z_keep(i + 2, u)

                for i in range(2, 6):
                    if b == 0 and i == 2:
                        act.wait_ge(nbsum_s, C - 1)
                        act.wait_ge(cps_done, 1)
                    if b and i == 2:
                        act.wait_ge(ts_done, n0)
                    if b and i == 4:
                        act.wait_ge(sl_ready, n0)
                        act.wait_ge(o_ready, n0)
                        for slot in range(2):
                            act.wait_ge(out_st[slot], 8 * n0)
                    p1_step(i, i % 2)
                    if b == 0 and i < 4:
                        high_parts("vo"[i - 2])
                with act.Fori(3, TILES // 2 - 1) as pair:
                    for u in range(2):
                        p1_step(pair * 2 + u, u)
                zT_high(TILES - 1, 1)
                exp_q(TILES - 3, 1)
                eT_keep(TILES - 4, 0)

                def exp_k(i, u):
                    act.wait_ge(ks_ready, n0 + i + 1)
                    a.activation(k32[:, i, :], k32[:, i, :], ACT.Exp).then_inc(ek_ready, 1)

                def z_high(i, u):
                    need(act, g_done, n0 + i - 1)
                    a.activation(z_h[:, u, :], z32[:, i, :], ACT.Copy).then_inc(zh_ready, 1)

                def film_high(c, u):
                    act.wait_ge(wf_in[u], 16 * (c - u) + 32)
                    need(act, film_mm, c)
                    if isinstance(c, int) and c == 0:
                        act.wait_ge(q_done, TILES)
                    for half, part in enumerate((z32, k32)):
                        a.activation(zT_h[:, half, :, :], part[:, u, :].rearrange("p (c t) -> p c t", c=C),
                                     ACT.Copy).then_inc(wf_high, 1)

                if b:
                    act.wait_ge(at_done, C * b)
                z_high(0, 0)
                z_high(1, 1)
                for i in range(3):
                    exp_k(i, i % 2)
                eT_keep(TILES - 3, 1)
                z_high(2, 0)
                exp_k(3, 1)
                z_high(3, 1)
                exp_q(TILES - 2, 0)
                exp_k(4, 0)
                z_high(4, 0)
                exp_k(5, 1)
                z_high(5, 1)
                eT_keep(TILES - 2, 0)
                exp_q(TILES - 1, 1)
                exp_k(6, 0)
                z_high(6, 0)
                eT_keep(TILES - 1, 1)
                if b == 0:
                    film_high(0, 0)
                exp_k(7, 1)
                z_high(7, 1)
                if b == 0:
                    film_high(1, 1)
                    with act.Fori(1, EC // 2) as pair:
                        for u in range(2):
                            exp_k(pair * 2 + (u + FILM_AT), u)
                            z_high(pair * 2 + (u + FILM_AT), u)
                            film_high(pair * 2 + u, u)
                with act.Fori((FILM_AT + EC) // 2 if b == 0 else 4, TILES // 2) as pair:
                    for u in range(2):
                        exp_k(pair * 2 + u, u)
                        z_high(pair * 2 + u, u)
                if b == 0:
                    act.wait_ge(film_mm, EC)
                    act.wait_ge(zl_ready, TILES - 2)
                    for half in range(2):
                        a.activation(film[:, half, :], PS[0:2 * B, 6 + half, :], ACT.Copy).then_inc(film_row, 1)

                def eT_high(i, u):
                    need(act, y_done, n0 + i - 1)
                    a.activation(zT_h[:, u, :, :], eq[:, i, :].rearrange("p (c t) -> p c t", c=C),
                                 ACT.Copy).then_inc(eTh_ready, 1)

                act.wait_ge(q_done, n0 + TILES)
                if b == 0:
                    act.wait_ge(film_mm, EC)
                for i in range(2):
                    eT_high(i, i)

                act.wait_ge(rden_ready, b + 1)
                if b:
                    act.wait_ge(xb_ready, n0)
                    act.wait_ge(o_ready, n0)

                def scale_g(j):
                    if j < C - 1:
                        act.wait_ge(g_blk, (C - 1) * b + j + 1)
                    else:
                        act.wait_ge(g_done, n0 + TILES)
                    if j >= 2:
                        act.wait_ge(gt_done, C * b + j - 1)
                    a.activation(Gn[:, j % 2, :], PS[:, j, :], ACT.Copy,
                                 scale=rden[:, j:j + 1]).then_inc(gn_ready, 1)

                def gt_high(j):
                    act.wait_ge(gt_done, C * b + j + 1)
                    if j >= 2:
                        act.wait_ge(at_done, C * b + j - 1)
                    else:
                        act.wait_ge(g_done, n0 + TILES)
                    a.activation(z_h[:, j % 2, :], PS[:, 4 + (j + 1) % 2, :], ACT.Copy).then_inc(gth_ready, 1)

                scale_g(0)
                for j in range(C):
                    if j + 1 < C:
                        scale_g(j + 1)
                    gt_high(j)

                def y_low(i, u):
                    act.wait_ge(y_done, n0 + i + 1)
                    need(act, y_evac, n0 + i - 1)
                    a.activation(y_lo[:, u, :].rearrange("p (k j c) -> p k j c", k=2, j=2), y_bank(u)[:, :, :, 1, :],
                                 ACT.Copy).then_inc(yb_s, 1)

                def next_zT(i):
                    act.wait_ge(t_done, n0 + TILES + i + 1)
                    act.wait_ge(y_done, n0 + TILES - 1 + i)
                    for half, signal in enumerate((z_kept, zTh_ready)):
                        cols = slice(half * C // 2, (half + 1) * C // 2)
                        a.activation(zT_h[:, i, cols, :],
                                     PS[:, 4 + i, half * D // 2:(half + 1) * D // 2].rearrange("p (c t) -> p c t", t=P),
                                     ACT.Copy).then_inc(signal, 1)

                def silu(i, u):
                    act.wait_ge(ts_done, n0 + i + 1)
                    if isinstance(i, int) and i == 0:
                        act.wait_ge(film_ready, 2)
                    need(act, sl_ready, n0 + i - 1)
                    for c in range(C):
                        a.activation(s32[:, u, c * P:(c + 1) * P], PS[:, 6, c * P:(c + 1) * P], ACT.Silu,
                                     bias=filmB[:, c, b:b + 1], scale=filmA[:, c, b:b + 1]).then_inc(silu_ready, 1)

                def s_high(i, u):
                    act.wait_ge(silu_ready, (i + n0 + 1) * C)
                    need(act, o_done, n0 + i - 1)
                    a.activation(ek_h[:, u, :], s32[:, u, :], ACT.Copy).then_inc(sh_ready, 1)

                pipeline(act, -3, TILES, *P4_LOOP, [(1, silu), (3, y_low), (1, s_high), (5, eT_high)],
                         {TILES - 3: b + 1 < B and (lambda: next_zT(0)),
                          TILES - 1: b + 1 < B and (lambda: next_zT(1))})

        @block.vector
        def _(dve):
            v = nc.vector
            v.memset(ones[:, :], 1.0).then_inc(consts, 1)

            def first_of_next(b, i):
                return b > 0 and isinstance(i, int) and i < 2

            def stats(b, i, u):
                slot = u
                if first_of_next(b, i):
                    dve.wait_ge(next_in[i], 16 * b)
                    slot = 2 + i
                else:
                    x_arrived(dve, b, i, u, False)
                v.bn_stats(bst[:, slot, :], z_at(b, i, u))
                dve.drain()
                v.bn_aggr(mv[:, slot, :], bst[:, slot, :]).then_inc(mv_ready, 1)

            def normalize(b, i, u):
                slot = 2 + i if first_of_next(b, i) else u
                dve.wait_ge(rstd_ready, b * TILES + i + 1)
                v.tensor_scalar(z_at(b, i, u), z_at(b, i, u), mv[:, slot, 0:1], rstd[:, slot:slot + 1],
                                ALU.subtract, ALU.mult).then_inc(z_ready, 1)

            def zT_low(b, i, u):
                dve.wait_ge(zTh_ready, b * TILES + i + 1)
                v.tensor_tensor(zT_l[:, u, :, :], PS[:, 4 + u, :].rearrange("p (c t) -> p c t", c=C),
                                zT_h[:, u, :, :].bitcast(F32), ALU.subtract).then_inc(zTl_ready, 1)

            def k_out(b, i, u, between=lambda: None):
                dve.wait_ge(k_done, b * TILES + i + 1)
                v.scalar_tensor_tensor(out=k32[:, i, :], in0=PS[:, u, :], scalar=mneg[:, b, bass.ds(i, 1)],
                                       in1=ck_b[:, :], op0=ALU.add, op1=ALU.add).then_inc(k_evac, 1)
                between()
                dve.wait_ge(k_evac, b * TILES + i + 1)
                if isinstance(i, int) and i == 0:
                    if b:
                        dve.wait_ge(den_done, b)
                    v.tensor_copy(colbuf[:, :], k32[:, 0, :]).then_inc(kmax_s, 1)
                else:
                    dve.wait_ge(kmax_s, b * TILES + i)
                    v.tensor_tensor(colbuf[:, :], colbuf[:, :], k32[:, i, :], ALU.max).then_inc(kmax_s, 1)

            def q_add(b, i, u):
                dve.wait_ge(q_done, b * TILES + i + 1)
                need(dve, qsub_s, b * TILES + i - 1)
                v.tensor_tensor(eq[:, i, :], PS[:, 2 + u, :], cq_b[:, :], ALU.add).then_inc(q_evac, 1)

            def q_max(b, i, u):
                v.tensor_reduce(qm[:, u, :], heads(eq[:, i, :]), axis=AX.X, op=ALU.max).then_inc(qmax_s, 1)

            def q_sum_heads(b, i, u):
                dve.wait_ge(eq_ready, b * TILES + i + 1)
                v.tensor_reduce(q_sum[:, u, :], heads(es[:, :]), axis=AX.X, op=ALU.add).then_inc(qsum_s, 1)

            def q_sum_invert(b, i, u):
                dve.wait_ge(qsum_s, b * TILES + i + 1)
                v.reciprocal(rq[:, u, :], q_sum[:, u, :]).then_inc(rq_s, 1)

            def low_parts(w, at):
                for c in range(C):
                    dve.wait_ge(w_high, C * at + c + 1)
                    if w == "o":
                        v.tensor_tensor(Wl[w][:, c, :], w_raw[w][:, c, :], Wh[w][:, c, :].bitcast(F32),
                                        ALU.subtract).then_inc(w_low, 1)
                    else:
                        v.scalar_tensor_tensor(out=Wl[w][:, c, :], in0=w_raw[w][:, c, :], scalar=ns_c[:, c:c + 1],
                                               in1=Wh[w][:, c, :].bitcast(F32), op0=ALU.mult,
                                               op1=ALU.subtract).then_inc(w_low, 1)

            stats(0, 0, 0)
            normalize(0, 0, 0)
            stats(0, 1, 1)
            dve.wait_ge(vecT, 1)
            v.tensor_copy(vec_c[:, 0:2 * C], PS[:, 7, 0:2 * C]).then_inc(vec_ready, 1)
            normalize(0, 1, 1)
            dve.wait_ge(vec_ready, 1)
            zT_low(0, 0, 0)
            low_parts("k", 0)
            zT_low(0, 1, 1)
            low_parts("q", 1)

            for b in range(B):
                n0 = b * TILES

                def q_out(i, u):
                    q_add(b, i, u)
                    dve.drain()
                    q_max(b, i, u)

                def k_stage(i, u):
                    k_out(b, i, u)

                def k_and_sums(i, u):
                    k_out(b, i, u, lambda: q_sum_heads(b, i - 1, 1 - u))
                    q_sum_invert(b, i - 1, 1 - u)

                if b == 0:
                    dve.wait_ge(mask_in, 16)
                    v.tensor_scalar(mneg[:, :, :], mask_i[:, :, :], 1.0, NEG, ALU.is_equal,
                                    ALU.mult).then_inc(mneg_s, 1)
                    stats(b, 2, 0)
                    for c in range(1, C):
                        dve.wait_ge(nbW_s, c + 1)
                        if c > 1:
                            dve.wait_ge(nbsum_s, c - 1)
                        v.tensor_tensor(nbW["k"][:, 0, :], nbW["k"][:, 0, :], nbW["k"][:, c, :],
                                        ALU.add).then_inc(nbsum_s, 1)
                    normalize(b, 2, 0)
                    dve.wait_ge(bkq_in, 32)
                    dve.wait_ge(cps_done, 1)
                    v.tensor_tensor(ck_b[:, :], PS[:, 6, :], bkq_b["k"], ALU.add).then_inc(ckq_s, 1)
                    dve.wait_ge(ckq_s, 1)
                    dve.wait_ge(mneg_s, 1)
                    k_stage(0, 0)
                    zT_low(b, 2, 0)
                    stats(b, 3, 1)
                    dve.wait_ge(cps_done, 2)
                    v.tensor_tensor(cq_b[:, :], PS[:, 7, :], bkq_b["q"], ALU.add).then_inc(ckq_s, 1)
                    dve.wait_ge(ckq_s, 2)
                    q_out(0, 0)
                if b:
                    stats(b, 3, 1)
                    zT_low(b, 2, 0)
                normalize(b, 3, 1)
                k_and_sums(1, 1)
                if b == 0:
                    zT_low(b, 3, 1)
                q_out(1, 1)

                def dve_step(i, u):
                    stats(b, i + 2, u)
                    zT_low(b, i + 1, 1 - u)
                    normalize(b, i + 2, u)
                    k_and_sums(i, u)
                    q_out(i, u)

                if b == 0:
                    stats(b, 4, 0)
                    normalize(b, 4, 0)
                    k_and_sums(2, 0)
                    q_out(2, 0)
                    stats(b, 5, 1)
                    dve.wait_ge(vecT, 2)
                    dve.wait_ge(cv_s, 1)
                    v.tensor_copy(vec_c[:, 2 * C:VROWS], PS[:, 5, C:C + VROWS - 2 * C]).then_inc(vec_ready, 1)
                    dve.wait_ge(vec_ready, 2)
                    v.tensor_tensor(cv_c[:, :], PS[:, 5, 0:C], bv_c[:, :], ALU.add).then_inc(cv_s, 1)
                    zT_low(b, 4, 0)
                    normalize(b, 5, 1)
                    k_and_sums(3, 1)
                    q_out(3, 1)
                    dve.wait_ge(emb_ready, B)
                    v.memset(emb_wide[:, :, :, :], 0.0).then_inc(emb_s1, 1)
                    v.tensor_copy(emb_hl[:, :, 0, :], emb_g[:, :, :]).then_inc(emb_s1, 1)
                    dve.wait_ge(emb_s1, 2)
                    v.tensor_tensor(emb_hl[:, :, 1, :], emb_g[:, :, :], emb_hl[:, :, 0, :].bitcast(F32),
                                    ALU.subtract).then_inc(emb_s1, 1)
                    v.tensor_copy(emb_hl[:, :, 2, :], emb_g[:, :, :]).then_inc(emb_s1, 1)
                    v.tensor_copy(emb_hl[:, :, 3, :], emb_wide[:, :, 0, :]).then_inc(emb_s1, 1)
                with dve.Fori(2 if b == 0 else 1, TILES // 2 - 1) as pair:
                    for u in range(2):
                        dve_step(pair * 2 + u, u)
                zT_low(b, TILES - 1, 1)
                k_and_sums(TILES - 2, 0)
                k_stage(TILES - 1, 1)

                dve.wait_ge(mt1, b + 1)
                v.tensor_reduce(mcol[:, :], PS[:, 4, :].rearrange("p (c t) -> p c t", c=C), axis=AX.X,
                                op=ALU.max).then_inc(mcol_s, 1)
                dve.wait_ge(mcol_s, b + 1)
                v.tensor_scalar(colbuf[:, :].rearrange("p (c t) -> p c t", c=C),
                                mcol[:, :].unsqueeze(2).broadcast_to([P, C, P]), MAX_FLOOR, None,
                                ALU.max).then_inc(mbig_s, 1)

                def k_shift(i, u):
                    v.tensor_tensor(k32[:, i, :], k32[:, i, :], M_b[:, :], ALU.subtract).then_inc(ks_ready, 1)

                def ek_split(i, u):
                    dve.wait_ge(ek_ready, n0 + i + 1)
                    need(dve, g_done, n0 + i - 1)
                    v.tensor_copy(ek_h[:, u, :], k32[:, i, :]).then_inc(ekh_s, 1)
                    dve.wait_ge(ekh_s, n0 + i + 1)
                    v.tensor_tensor(ek_l[:, u, :], k32[:, i, :], ek_h[:, u, :].bitcast(F32),
                                    ALU.subtract).then_inc(ekl_ready, 1)

                def film_low(c, u):
                    dve.wait_ge(wf_high, (c + 1) * 2)
                    v.tensor_tensor(zT_l[:, 0, :, :], z32[:, u, :].rearrange("p (c t) -> p c t", c=C),
                                    zT_h[:, 0, :, :].bitcast(F32), ALU.subtract)
                    v.tensor_tensor(zT_l[:, 1, :, :], k32[:, u, :].rearrange("p (c t) -> p c t", c=C),
                                    zT_h[:, 1, :, :].bitcast(F32), ALU.subtract).then_inc(wf_low, 1)
                    v.tensor_copy(emb_now[:, u, :], emb_hl[:, c, :, :].bitcast(F32)
                                  .rearrange("p k b -> p (k b)")).then_inc(embT_ready, 1)

                dve.wait_ge(mt2, b + 1)
                k_shift(0, 0)
                k_shift(1, 1)
                if b:
                    dve.wait_ge(o_done, n0)
                ek_split(0, 0)
                q_add(b, TILES - 2, 0)
                q_add(b, TILES - 1, 1)
                ek_split(1, 1)
                k_shift(2, 0)
                k_shift(3, 1)
                for i, u in ((2, 0), (3, 1)):
                    tile = TILES - 4 + i
                    dve.wait_ge(q_evac, n0 + tile + 1)
                    q_max(b, tile, u)
                    ek_split(i, u)
                    dve.wait_ge(qmax_s, n0 + tile + 1)
                    v.tensor_tensor(heads(eq[:, tile, :]), heads(eq[:, tile, :]), per_head(qm[:, u, :]),
                                    ALU.subtract).then_inc(qsub_s, 1)
                    k_shift(i + 2, u)

                def q_softmax(i, u):
                    q_sum_heads(b, i, u)
                    q_sum_invert(b, i, u)
                    dve.wait_ge(rq_s, n0 + i + 1)
                    v.tensor_tensor(heads(es[:, :]), heads(es[:, :]), per_head(rq[:, u, :]),
                                    ALU.mult).then_inc(en_ready, 1)

                q_softmax(TILES - 2, 0)
                for i in range(4, 6):
                    ek_split(i, i % 2)
                    k_shift(i + 2, i % 2)
                q_softmax(TILES - 1, 1)
                if b == 0:
                    with dve.Fori(0, EC // 2) as pair:
                        for u in range(2):
                            ek_split(pair * 2 + (u + FILM_AT), u)
                            k_shift(pair * 2 + (u + FILM_AT + 2), u)
                            film_low(pair * 2 + u, u)
                else:
                    with dve.Fori(3, TILES // 2 - 1) as pair:
                        for u in range(2):
                            ek_split(pair * 2 + u, u)
                            k_shift(pair * 2 + (u + 2), u)
                ek_split(TILES - 2, 0)
                ek_split(TILES - 1, 1)

                def eT_low(i, u):
                    dve.wait_ge(eTh_ready, n0 + i + 1)
                    v.tensor_tensor(zT_l[:, u, :, :], eq[:, i, :].rearrange("p (c t) -> p c t", c=C),
                                    zT_h[:, u, :, :].bitcast(F32), ALU.subtract).then_inc(eTl_ready, 1)

                for i in range(2):
                    eT_low(i, i)

                dve.wait_ge(den_done, b + 1)
                v.reciprocal(rden[:, :], PS[:, 4, 0:C]).then_inc(rden_ready, 1)
                for j in range(C):
                    dve.wait_ge(gth_ready, C * b + j + 1)
                    v.tensor_tensor(z_l[:, j % 2, :], PS[:, 4 + (j + 1) % 2, :], z_h[:, j % 2, :].bitcast(F32),
                                    ALU.subtract).then_inc(gtl_ready, 1)
                    if j:
                        attn_out(j - 1)

                    def attn_out(j):
                        dve.wait_ge(at_done, C * b + j + 1)
                        v.scalar_tensor_tensor(
                            out=R32[:, j, :], in0=PS[:, j, 0:P], scalar=cv_c[:, j:j + 1],
                            in1=same_head[:, :, :].rearrange("p h d -> p (h d)"), op0=ALU.add,
                            op1=ALU.mult).then_inc(r32_s, 1)
                        dve.wait_ge(r32_s, C * b + j + 1)
                        if b and j == 0:
                            dve.wait_ge(y_done, n0)
                        v.tensor_copy(R_hl[:, j, 0, :], R32[:, j, :]).then_inc(rh_s, 1)
                        dve.wait_ge(rh_s, C * b + j + 1)
                        v.tensor_tensor(R_hl[:, j, 1, :], R32[:, j, :], R_hl[:, j, 0, :].bitcast(F32),
                                        ALU.subtract).then_inc(r_ready, 1)
                attn_out(C - 1)
                if b == 0:
                    dve.wait_ge(filmT, 1)
                    fT = PS[:, 6, 0:2 * C * 2 * B].rearrange("p (c k b) -> p c k b", k=2, b=B)
                    v.tensor_tensor(filmT_s[:, :, :], fT[:, :, 0, :],
                                    bf_c.unsqueeze(2).broadcast_to([P, 2 * C, B]), ALU.add).then_inc(film_out, 1)
                    dve.wait_ge(film_out, 1)
                    v.tensor_tensor(filmT_s[:, :, :], filmT_s[:, :, :], fT[:, :, 1, :], ALU.add).then_inc(film_out, 1)
                    dve.wait_ge(film_out, 2)
                    v.scalar_tensor_tensor(out=filmA[:, :, :], in0=filmT_s[:, 0:C, :], scalar=1.0,
                                           in1=fs_c.unsqueeze(2).broadcast_to([P, C, B]), op0=ALU.add,
                                           op1=ALU.mult).then_inc(film_ready, 1)
                    v.scalar_tensor_tensor(out=filmB[:, :, :], in0=filmT_s[:, 0:C, :], scalar=1.0,
                                           in1=fb_c.unsqueeze(2).broadcast_to([P, C, B]), op0=ALU.add,
                                           op1=ALU.mult).then_inc(film_out, 1)
                    dve.wait_ge(film_out, 3)
                    v.tensor_tensor(filmB[:, :, :], filmB[:, :, :], filmT_s[:, C:2 * C, :],
                                    ALU.add).then_inc(film_ready, 1)

                def y_out(i, u):
                    dve.wait_ge(yb_s, n0 + i + 1)
                    v.tensor_tensor(y32[:, u, :].rearrange("p (k j c) -> p k j c", k=2, j=2), y_bank(u)[:, :, :, 0, :],
                                    y_lo[:, u, :].rearrange("p (k j c) -> p k j c", k=2, j=2),
                                    ALU.add).then_inc(y_evac, 1)
                    dve.wait_ge(y_evac, n0 + i + 1)
                    v.bn_stats(bst[:, u, :], y32[:, u, :])
                    dve.drain()
                    v.bn_aggr(mv[:, u, :], bst[:, u, :]).then_inc(mv2_ready, 1)

                def y_norm(i, u):
                    need(dve, ts_done, n0 + i - 1)
                    dve.wait_ge(rstd2_ready, n0 + i + 1)
                    v.tensor_scalar(yn[:, u, :], y32[:, u, :], mv[:, u, 0:1], rstd[:, u:u + 1], ALU.subtract,
                                    ALU.mult).then_inc(yn_ready, 1)

                def result(i, u):
                    dve.wait_ge(o_done, n0 + i + 1)
                    dve.wait_ge(xb_ready, n0 + i + 1)
                    if not isinstance(i, int) or n0 + i >= 2:
                        dve.wait_ge(out_st[u], 8 * (n0 + i - u))
                    v.tensor_tensor(ob[:, u, :], PS[:, 5 + 2 * u, :], xb[:, u, :], ALU.add).then_inc(o_ready, 1)

                more = b + 1 < B
                pipeline(dve, -3, TILES - 3, *P4_LOOP, [(-1, result), (2, y_norm), (3, y_out), (5, eT_low)],
                         {TILES - 4: more and (lambda: stats(b + 1, 0, 0))})
                if more:
                    normalize(b + 1, 0, 0)
                result(TILES - 4, 0)
                y_norm(TILES - 1, 1)

                def s_low_last(i, u):
                    dve.wait_ge(sh_ready, n0 + i + 1)
                    dve.wait_ge(sl_ready, n0 + i)
                    v.tensor_tensor(ek_l[:, u, :], s32[:, u, :], ek_h[:, u, :].bitcast(F32),
                                    ALU.subtract).then_inc(sl_ready, 1)

                if more:
                    stats(b + 1, 1, 1)
                    zT_low(b + 1, 0, 0)
                if not more:
                    s_low_last(TILES - 2, 0)
                result(TILES - 3, 1)
                if not more:
                    s_low_last(TILES - 1, 1)
                if more:
                    dve.wait_ge(acc_s, n0 + TILES)
                    k_out(b + 1, 0, 0)
                    normalize(b + 1, 1, 1)
                result(TILES - 2, 0)
                if more:
                    stats(b + 1, 2, 0)
                    dve.wait_ge(eTl_ready, n0 + TILES)
                    q_add(b + 1, 0, 0)
                    normalize(b + 1, 2, 0)
                    zT_low(b + 1, 1, 1)
                    dve.wait_ge(q_evac, n0 + TILES + 1)
                    q_max(b + 1, 0, 0)
                result(TILES - 1, 1)

        @block.tensor
        def _(pe):
            def three(out_ps, lh, ll, rh, rl, start, stop):
                nc.tensor.matmul(out_ps, lh, rh, start=start, stop=False)
                nc.tensor.matmul(out_ps, lh, rl, start=False, stop=False)
                return nc.tensor.matmul(out_ps, ll, rh, start=False, stop=stop)

            def transposes(bank, src):
                for c in range(C):
                    last = nc.tensor.transpose(PS[:, bank, c * P:(c + 1) * P], src[:, c * P:(c + 1) * P], ident[:, :])
                return last

            def bias_rows(n, w, bank):
                pe.wait_ge(nbsum_s, (n + 1) * (C - 1))
                nc.tensor.matmul(PS[:, bank, :], ones[:, :], nbW[w][:, 0, :], start=True,
                                 stop=True).then_inc(cps_done, 1)

            def transpose_z(b, i, u):
                pe.wait_ge(z_ready, b * TILES + i + 1)
                need(pe, zTl_ready, b * TILES + i - 1)
                transposes(4 + u, z_at(b, i, u)).then_inc(t_done, 1)

            pe.wait_ge(ident_s, 2)
            pe.wait_ge(vec01_in, 32)
            nc.tensor.transpose(PS[:, 7, 0:2 * C], vec_rows, ident[0:2 * C, 0:2 * C]).then_inc(vecT, 1)
            transpose_z(0, 0, 0)

            for b in range(B):
                n0 = b * TILES

                def project_k(i, u):
                    pe.wait_ge(zTl_ready, n0 + i + 1)
                    need(pe, k_evac, n0 + i - 1)
                    for c in range(C):
                        last = three(PS[:, u, :], zT_h[:, u, c, :], zT_l[:, u, c, :], Wh["k"][:, c, :],
                                     Wl["k"][:, c, :], c == 0, c == C - 1)
                    last.then_inc(k_done, 1)

                def project_q(i, u, part=slice(0, C)):
                    if part.start == 0:
                        need(pe, q_evac, n0 + i - 1)
                    for c in range(part.start, part.stop):
                        if b == 0 and isinstance(i, int) and i == 0:
                            pe.wait_ge(w_low, C + c + 1)
                        last = three(PS[:, 2 + u, :], zT_h[:, u, c, :], zT_l[:, u, c, :], Wh["q"][:, c, :],
                                     Wl["q"][:, c, :], c == 0, c == C - 1)
                    if part.stop == C:
                        last.then_inc(q_done, 1)

                def transpose_e(i, u):
                    pe.wait_ge(en_ready, n0 + i + 1)
                    need(pe, te_kept, n0 + i - 1)
                    transposes(6 + u, es[:, :]).then_inc(te_done, 1)

                if b == 0:
                    transpose_z(0, 1, 1)
                    for c in range(C):
                        pe.wait_ge(w_low, c + 1)
                        if c == 0:
                            pe.wait_ge(zTl_ready, 1)
                        last = three(PS[:, 0, :], zT_h[:, 0, c, :], zT_l[:, 0, c, :], Wh["k"][:, c, :],
                                     Wl["k"][:, c, :], c == 0, c == C - 1)
                    last.then_inc(k_done, 1)
                    project_q(0, 0)
                    pe.wait_ge(consts, 1)
                    project_k(1, 1)
                    bias_rows(0, "k", 6)
                    transpose_z(0, 2, 0)
                    project_q(1, 1)
                    bias_rows(1, "q", 7)
                else:
                    project_k(1, 1)
                    transpose_z(b, 2, 0)
                    project_q(1, 1)
                    pe.wait_ge(o_ready, n0)
                    pe.wait_ge(silu_ready, C * n0)

                def p1_step(i, u):
                    transpose_z(b, i + 1, 1 - u)
                    project_k(i, u)
                    transpose_e(i - 2, u)
                    project_q(i, u)

                for i in range(2, 4):
                    project_k(i, i % 2)
                    transpose_z(b, i + 1, 1 - i % 2)
                    project_q(i, i % 2)
                    if b == 0 and i == 3:
                        pe.wait_ge(zTl_ready, 4)
                        pe.wait_ge(vec_in, 16 * (len(VECS) - 2))
                        rest = VROWS - 2 * C
                        nc.tensor.transpose(PS[:, 5, C:C + rest], vec_rest, ident[0:rest, 0:rest]).then_inc(vecT, 1)
                        pe.wait_ge(nbsum_s, 3 * (C - 1))
                        for j in range(C):
                            last = nc.tensor.matmul(PS[:, 5, j:j + 1], nbW["v"][:, 0, j * P:(j + 1) * P],
                                                    ones[:, 0:1], start=True, stop=True)
                        last.then_inc(cv_s, 1)
                    transpose_e(i - 2, i % 2)
                    if b == 0 and i == 3:
                        pe.wait_ge(cv_s, 2)
                with pe.Fori(2, TILES // 2 - 1) as pair:
                    for u in range(2):
                        p1_step(pair * 2 + u, u)
                transpose_z(b, TILES - 1, 1)
                project_k(TILES - 2, 0)
                transpose_e(TILES - 4, 0)
                project_k(TILES - 1, 1)
                project_q(TILES - 2, 0, slice(0, C // 2))

                pe.wait_ge(kmax_s, n0 + TILES)
                transposes(4, colbuf[:, :]).then_inc(mt1, 1)
                project_q(TILES - 2, 0, slice(C // 2, C))
                pe.wait_ge(mbig_s, b + 1)
                transposes(5, colbuf[:, :]).then_inc(mt2, 1)
                project_q(TILES - 1, 1)
                transpose_e(TILES - 3, 1)

                def gram(i, u, first=False, final=False):
                    pe.wait_ge(ekl_ready, n0 + i + 1)
                    pe.wait_ge(zl_ready, n0 + i + 1)
                    for j in range(C):
                        cols = slice(j * P, (j + 1) * P)
                        if first and j >= 2:
                            pe.wait_ge(q_evac, n0 + TILES - 3 + j)
                        last = three(PS[:, j, :], ek_h[:, u, cols], ek_l[:, u, cols], z_h[:, u, :], z_l[:, u, :],
                                     first, final)
                        if final and j < C - 1:
                            last.then_inc(g_blk, 1)
                        if final and j == 1:
                            sum_rows()
                    last.then_inc(g_done, 1)

                def sum_rows():
                    pe.wait_ge(acc_s, n0 + TILES)
                    pe.wait_ge(consts, 1)
                    for j in range(C):
                        last = nc.tensor.matmul(PS[:, 4, j:j + 1], colbuf[:, j * P:(j + 1) * P], ones[:, 0:1],
                                                start=True, stop=True)
                    last.then_inc(den_done, 1)

                def film_rows(c, u):
                    pe.wait_ge(wf_low, c + 1)
                    pe.wait_ge(embT_ready, c + 1)
                    if isinstance(c, int) and c == 0:
                        pe.wait_ge(te_kept, TILES)
                    for half in range(2):
                        rows = PS[0:2 * B, 6 + half, :]
                        nc.tensor.matmul(rows, emb_now[:, u, 0:2 * B],
                                         zT_h[:, half, :, :].rearrange("p c t -> p (c t)"), start=is_first(c), stop=False)
                        last = nc.tensor.matmul(rows, emb_now[:, u, 2 * B:4 * B],
                                                zT_l[:, half, :, :].rearrange("p c t -> p (c t)"), start=False, stop=is_last(c))
                    last.then_inc(film_mm, 1)

                def is_first(c):
                    return isinstance(c, int) and c == 0

                def is_last(c):
                    return isinstance(c, int) and c == EC - 1

                gram(0, 0, first=True)
                for i in range(1, 4):
                    gram(i, i % 2)
                transpose_e(TILES - 2, 0)
                for i in range(4, 6):
                    gram(i, i % 2)
                transpose_e(TILES - 1, 1)
                if b == 0:
                    for c in range(2):
                        gram(c + FILM_AT, c)
                        film_rows(c, c)
                    with pe.Fori(1, EC // 2 - 1) as pair:
                        for u in range(2):
                            gram(pair * 2 + (u + FILM_AT), u)
                            film_rows(pair * 2 + u, u)
                    for c in range(EC - 2, EC):
                        gram(c + FILM_AT, c % 2)
                        film_rows(c, c % 2)
                else:
                    with pe.Fori(3, TILES // 2 - 1) as pair:
                        for u in range(2):
                            gram(pair * 2 + u, u)
                gram(TILES - 2, 0)
                gram(TILES - 1, 1, final=True)

                def transpose_g(j):
                    pe.wait_ge(gn_ready, C * b + j + 1)
                    if j >= 2:
                        pe.wait_ge(gtl_ready, C * b + j - 1)
                    transposes(4 + (j + 1) % 2, Gn[:, j % 2, :]).then_inc(gt_done, 1)

                transpose_g(0)
                for j in range(C):
                    if j + 1 < C:
                        transpose_g(j + 1)
                    if b == 0 and j == 0:
                        pe.wait_ge(film_row, 2)
                        for c in range(2 * C):
                            last = nc.tensor.transpose(PS[:, 6, c * 2 * B:(c + 1) * 2 * B],
                                                       film[:, c // C, (c % C) * P:(c % C + 1) * P],
                                                       ident[0:2 * B, 0:2 * B])
                        last.then_inc(filmT, 1)
                    pe.wait_ge(gtl_ready, C * b + j + 1)
                    pe.wait_ge(wv_low, C)
                    cols = slice(j * P, (j + 1) * P)
                    for c in range(C):
                        rows = slice(c * P, (c + 1) * P)
                        last = three(PS[:, j, 0:P], Wh["v"][:, c, cols], Wl["v"][:, c, cols], z_h[:, j % 2, rows],
                                     z_l[:, j % 2, rows], c == 0, c == C - 1)
                    last.then_inc(at_done, 1)

                def attend(i, u):
                    pe.wait_ge(eTl_ready, n0 + i + 1)
                    need(pe, y_evac, n0 + i - 1)
                    for j in range(C):
                        if isinstance(i, int) and i < 2:
                            pe.wait_ge(r_ready, C * b + j + 1)
                            if j < 2:
                                pe.wait_ge(r32_s, C * b + (4 if i else 2))
                        y_ps = y_bank(u)[:, j // 2, j % 2, :, :]
                        nc.tensor.matmul(y_ps, zT_h[:, u, j, :], R_hl[:, j, :, :], start=True, stop=False)
                        last = nc.tensor.matmul(y_ps[:, 0, :], zT_l[:, u, j, :], R_hl[:, j, 0, :], start=False,
                                                stop=True)
                    last.then_inc(y_done, 1)

                def transpose_y(i, u):
                    pe.wait_ge(yn_ready, n0 + i + 1)
                    need(pe, silu_ready, (i + n0) * C)
                    if b == 0 and isinstance(i, int) and i == 0:
                        pe.wait_ge(film_out, 2)
                    transposes(6, yn[:, u, :]).then_inc(ts_done, 1)

                def project_out(i, u):
                    pe.wait_ge(sl_ready, n0 + i + 1)
                    if b == 0 and isinstance(i, int) and i == 0:
                        pe.wait_ge(wv_low, 2 * C)
                    need(pe, o_ready, n0 + i - 1)
                    for c in range(C):
                        cols = slice(c * P, (c + 1) * P)
                        last = three(PS[:, 5 + 2 * u, :], ek_h[:, u, cols], ek_l[:, u, cols], Wh["o"][:, c, :],
                                     Wl["o"][:, c, :], c == 0, c == C - 1)
                    last.then_inc(o_done, 1)

                attend(0, 0)
                attend(1, 1)
                for _ in range(KEEP_WARM):
                    nc.tensor.matmul(PS[:, 4, :], Wh["q"][:, 0, 0:P], Wh["q"][:, 0, :], start=True, stop=True)
                transpose_y(0, 0)
                attend(2, 0)
                pipeline(pe, 0, TILES - 3, *P4_LOOP, [(1, transpose_y), (3, attend), (0, project_out)])
                more = b + 1 < B
                if more:
                    transpose_z(b + 1, 0, 0)
                transpose_y(TILES - 2, 0)
                project_out(TILES - 3, 1)
                if more:
                    pe.wait_ge(y_evac, n0 + TILES - 1)
                    project_k(TILES, 0)
                transpose_y(TILES - 1, 1)
                project_out(TILES - 2, 0)
                if more:
                    pe.wait_ge(y_evac, n0 + TILES)
                    project_q(TILES, 0)
                    pe.wait_ge(o_ready, n0 + TILES - 1)
                    transpose_z(b + 1, 1, 1)
                project_out(TILES - 1, 1)


_INS = ["x", "cond_2048", "mask_BxS_ik0", "L0_cond_norm_scale", "L0_cond_norm_bias", "L0_cond_Wq", "L0_cond_bq",
        "L0_cond_Wk", "L0_cond_bk", "L0_cond_Wv", "L0_cond_bv", "L0_cond_film_emb_W", "L0_cond_film_emb_b",
        "L0_cond_film_norm_scale", "L0_cond_film_norm_bias", "L0_cond_film_out_W", "L0_cond_film_out_b"]


def kernel(**inputs):
    import numpy as _np
    import concourse.bacc as _bacc
    from concourse.bass_utils import run_bass_kernel_spmd as _run

    nc = _bacc.Bacc("TRN2", target_bir_lowering=False, num_devices=1)
    arrays, args = {}, []
    for name in _INS:
        arr = _np.ascontiguousarray(inputs[name])
        arrays[f"in_{name}"] = arr
        args.append(nc.dram_tensor(f"in_{name}", arr.shape, mybir.dt.from_np(arr.dtype), kind="ExternalInput").ap())
    out = nc.dram_tensor("out_0", inputs["x"].shape, F32, kind="ExternalOutput").ap()
    cond_block(nc, *args, out)
    r = _run(nc, [arrays], core_ids=[0])
    return r.results[0]["out_0"]
```
